# Optimizing a Trainium2 kernel written in Bass

```python
import numpy as np
import jax
import jax.numpy as jnp

def _softmax(x, axis=-1):
    return jax.nn.softmax(x, axis=axis)

def _gelu(x):
    return jax.nn.gelu(x, approximate=True)

def _silu(x):
    return jax.nn.silu(x)

def _sigmoid(x):
    return jax.nn.sigmoid(x)

def _layernorm(x, axis=-1, eps=1e-05):
    m = jnp.mean(x, axis=axis, keepdims=True)
    v = jnp.var(x, axis=axis, keepdims=True)
    return (x - m) / jnp.sqrt(v + eps)

def _scatter_add(tgt, idx, src, axis=0):
    return tgt.at[idx].add(src)

def _segment_sum(src, seg, n):
    return jax.ops.segment_sum(src, seg, n)
kernel_name = 'mk_cond_seq_d1_seqx_r2_1c16f7'

def setup_inputs(seed: int=0):
    np.random.seed(seed)
    _w = jnp.asarray

    def _rec_inputs():
        import jax
        import jax.numpy as jnp
        _rk = jax.random.key(seed)
        x = 7.22e-05 + 1 * jax.random.normal(jax.random.fold_in(_rk, 1), (16, 512, 512), jnp.float32)
        _lenS = 512 - jax.random.randint(jax.random.fold_in(_rk, 7), (16,), 0, max(1, 512 // 4) + 1, jnp.int32)
        _lenS2 = 512 - jax.random.randint(jax.random.fold_in(_rk, 8), (16,), 0, max(1, 512 // 4) + 1, jnp.int32)
        condB_gatescore = jax.random.uniform(jax.random.fold_in(_rk, 11), (16,), jnp.float32, 0.0, 0.581427)
        return (x, condB_gatescore)
    x, condB_gatescore = _rec_inputs()

    def _L0_cond_setup():
        import jax, jax.numpy as jnp
        import numpy as np
        D_MODEL = 512
        N_HEADS = 16
        D_HEAD = D_MODEL // N_HEADS
        D_FF = 2048
        EPS = 1e-05

        def layernorm(x, gamma, beta):
            mu = jnp.mean(x, axis=-1, keepdims=True)
            var = jnp.var(x, axis=-1, keepdims=True)
            return (x - mu) * jax.lax.rsqrt(var + EPS) * gamma + beta
        key = jax.random.key(seed)
        ks = jax.random.split(key, 16)
        B, T = (4, 1024)
        s = 1.0 / np.sqrt(D_MODEL)
        sf = 1.0 / np.sqrt(D_FF)
        return {'x': jax.random.normal(ks[0], (B, T, D_MODEL), jnp.float32), 'gate_score': jax.random.uniform(ks[1], (B,), jnp.float32), 'Wq': jax.random.normal(ks[2], (D_MODEL, D_MODEL), jnp.float32) * s, 'bq': jnp.zeros((D_MODEL,), jnp.float32), 'Wk': jax.random.normal(ks[3], (D_MODEL, D_MODEL), jnp.float32) * s, 'bk': jnp.zeros((D_MODEL,), jnp.float32), 'Wv': jax.random.normal(ks[4], (D_MODEL, D_MODEL), jnp.float32) * s, 'bv': jnp.zeros((D_MODEL,), jnp.float32), 'Wo': jax.random.normal(ks[5], (D_MODEL, D_MODEL), jnp.float32) * s, 'bo': jnp.zeros((D_MODEL,), jnp.float32), 'W1': jax.random.normal(ks[6], (D_MODEL, D_FF), jnp.float32) * s, 'b1': jnp.zeros((D_FF,), jnp.float32), 'W2': jax.random.normal(ks[7], (D_FF, D_MODEL), jnp.float32) * sf, 'b2': jnp.zeros((D_MODEL,), jnp.float32), 'gamma1': jnp.ones((D_MODEL,), jnp.float32), 'beta1': jnp.zeros((D_MODEL,), jnp.float32), 'gamma2': jnp.ones((D_MODEL,), jnp.float32), 'beta2': jnp.zeros((D_MODEL,), jnp.float32)}
    _L0_cond_all = _L0_cond_setup()
    _L0_cond_in = {k: v for k, v in _L0_cond_all.items() if k in ('Wq', 'bq', 'Wk', 'bk', 'Wv', 'bv', 'Wo', 'bo', 'W1', 'b1', 'W2', 'b2', 'gamma1', 'beta1', 'gamma2', 'beta2')}
    del _L0_cond_all
    return {'x': x, 'condB_gatescore': condB_gatescore, 'L0_cond_Wq': _L0_cond_in['Wq'], 'L0_cond_bq': _L0_cond_in['bq'], 'L0_cond_Wk': _L0_cond_in['Wk'], 'L0_cond_bk': _L0_cond_in['bk'], 'L0_cond_Wv': _L0_cond_in['Wv'], 'L0_cond_bv': _L0_cond_in['bv'], 'L0_cond_Wo': _L0_cond_in['Wo'], 'L0_cond_bo': _L0_cond_in['bo'], 'L0_cond_W1': _L0_cond_in['W1'], 'L0_cond_b1': _L0_cond_in['b1'], 'L0_cond_W2': _L0_cond_in['W2'], 'L0_cond_b2': _L0_cond_in['b2'], 'L0_cond_gamma1': _L0_cond_in['gamma1'], 'L0_cond_beta1': _L0_cond_in['beta1'], 'L0_cond_gamma2': _L0_cond_in['gamma2'], 'L0_cond_beta2': _L0_cond_in['beta2']}

def reference(x, condB_gatescore, L0_cond_Wq, L0_cond_bq, L0_cond_Wk, L0_cond_bk, L0_cond_Wv, L0_cond_bv, L0_cond_Wo, L0_cond_bo, L0_cond_W1, L0_cond_b1, L0_cond_W2, L0_cond_b2, L0_cond_gamma1, L0_cond_beta1, L0_cond_gamma2, L0_cond_beta2):
    import jax
    import jax.numpy as jnp

    def _L0_cond_ref(x, gate_score, Wq, bq, Wk, bk, Wv, bv, Wo, bo, W1, b1, W2, b2, gamma1, beta1, gamma2, beta2):
        import jax, jax.numpy as jnp
        import numpy as np
        D_MODEL = 512
        N_HEADS = 16
        D_HEAD = D_MODEL // N_HEADS
        D_FF = 2048
        EPS = 1e-05

        def layernorm(x, gamma, beta):
            mu = jnp.mean(x, axis=-1, keepdims=True)
            var = jnp.var(x, axis=-1, keepdims=True)
            return (x - mu) * jax.lax.rsqrt(var + EPS) * gamma + beta
        B, T, C = x.shape
        h = layernorm(x, gamma1, beta1)
        Q = (h @ Wq + bq).reshape(B, T, N_HEADS, D_HEAD).transpose(0, 2, 1, 3)
        K = (h @ Wk + bk).reshape(B, T, N_HEADS, D_HEAD).transpose(0, 2, 1, 3)
        V = (h @ Wv + bv).reshape(B, T, N_HEADS, D_HEAD).transpose(0, 2, 1, 3)
        scores = jnp.einsum('bhqd,bhkd->bhqk', Q, K) / np.sqrt(D_HEAD)
        causal = jnp.tril(jnp.ones((T, T), dtype=bool))
        scores = jnp.where(causal, scores, -jnp.inf)
        attn = jax.nn.softmax(scores, axis=-1)
        ctx = jnp.einsum('bhqk,bhkd->bhqd', attn, V)
        ctx = ctx.transpose(0, 2, 1, 3).reshape(B, T, C)
        attn_out = ctx @ Wo + bo
        x1 = x + attn_out
        h2 = layernorm(x1, gamma2, beta2)
        ff = jax.nn.gelu(h2 @ W1 + b1, approximate=False) @ W2 + b2
        x2 = x1 + ff
        g = gate_score[:, None, None]
        return x + g * (x2 - x)
    x = _L0_cond_ref(x, condB_gatescore, L0_cond_Wq, L0_cond_bq, L0_cond_Wk, L0_cond_bk, L0_cond_Wv, L0_cond_bv, L0_cond_Wo, L0_cond_bo, L0_cond_W1, L0_cond_b1, L0_cond_W2, L0_cond_b2, L0_cond_gamma1, L0_cond_beta1, L0_cond_gamma2, L0_cond_beta2)
    return x

_drawn_inputs = setup_inputs


def setup_inputs(seed=0):
    import zlib

    import numpy as np

    out = dict(_drawn_inputs(seed))
    spreads = {'L0_cond_bq': (0.0, 0.8),
     'L0_cond_bk': (0.0, 0.8),
     'L0_cond_bv': (0.0, 0.1),
     'L0_cond_bo': (0.0, 0.1),
     'L0_cond_b1': (0.0, 0.336),
     'L0_cond_b2': (0.0, 0.1),
     'L0_cond_gamma1': (1.0, 0.6),
     'L0_cond_beta1': (0.0, 0.1),
     'L0_cond_gamma2': (1.0, 0.2),
     'L0_cond_beta2': (0.0, 0.341)}
    factors = {}
    for name, (base, spread) in spreads.items():
        noise = np.random.default_rng([zlib.crc32(name.encode()), seed]).standard_normal(out[name].shape)
        drawn = base * np.exp(spread * noise) if base else spread * noise
        out[name] = jnp.asarray(drawn.astype(out[name].dtype))
    for name, factor in factors.items():
        out[name] = (out[name] * factor).astype(out[name].dtype)
    return out
```

```python
from contextlib import ExitStack

import concourse.bass as bass
from concourse import mybir

ALU = mybir.AluOpType
ACT = mybir.ActivationFunctionType
AX_X = mybir.AxisListType.X
F32 = mybir.dt.float32
F16 = mybir.dt.float16
BF16 = mybir.dt.bfloat16

P = 128
T, C, NH, FF = 512, 512, 16, 2048
DH = C // NH
TT = T // P
DK = C // P
FJ = FF // P
HPT = P // DH
PARTS = 3
EPS = 1e-5
NORM_TO = 1024.0
TINY = 1e-12
LOG_P = 6.931471805599453
MASKED = -1e30

COLS, CONSTS = 11, 9
H2_AT = 5

GROUPS = [(qt, h0, max(1, TT // (qt + 1) if qt < 2 else 1))
          for qt in range(TT) for h0 in range(0, NH, max(1, TT // (qt + 1) if qt < 2 else 1))]
NG = len(GROUPS)
FIRST = [min(g for g, x in enumerate(GROUPS) if x[0] == qt) for qt in range(TT)]
LAST = [max(g for g, x in enumerate(GROUPS) if x[0] == qt) for qt in range(TT)]
STEPS = NG + 5

F_MMS, W_MMS = 3 * FJ, 3 * DK
DENSE = [(kind, t, n) for t in range(TT) for kind, m in (("F", F_MMS), ("W", W_MMS)) for n in range(m)
         if (kind, t) != ("W", TT - 1)]
QUOTA = [5] * 28 + [4] * 17 + [6, 6, 6, 2]
assert sum(QUOTA) == len(DENSE) and len(QUOTA) == STEPS
CUT = [sum(QUOTA[:s]) for s in range(STEPS + 1)]


def step_of(kind, t):
    at = max(n for n, x in enumerate(DENSE) if x[:2] == (kind, t))
    return max(s for s in range(STEPS) if CUT[s] <= at)


CTX_EVAC = {LAST[qt] + 4: qt for qt in range(TT)}
Z_T = {5: 0, 13: 1, 24: 2, 36: 3}
F_EVAC = {step_of("F", t) + 1: t for t in range(TT)}
W_EVAC = {step_of("W", t) + 1: t for t in range(TT - 1)}
OTHERS = [[] for _ in range(STEPS)]
for _s in range(STEPS):
    if _s - 1 in CTX_EVAC:
        OTHERS[_s].append(("ctx", CTX_EVAC[_s - 1]))
    if _s in Z_T:
        OTHERS[_s].append(("z", Z_T[_s]))
for _s, _t in W_EVAC.items():
    OTHERS[next(s for s in range(_s + 4, STEPS) if not OTHERS[s])].append(("h2", _t))
assert max(map(len, OTHERS)) == 1
ROWS_AT = [[("h2", W_EVAC.get(s - 1))] * (s - 1 in W_EVAC) + [("z", Z_T.get(s + 2))] * (s + 2 in Z_T)
           for s in range(STEPS)]
SETUP_1, SETUP_2 = 10, 28
_ORDER = [job for s in range(STEPS) for job in [("p", s - 1)] * (1 <= s <= NG) + OTHERS[s]]
PLACE = {("h2", TT - 1): 0} | {job: n + 1 for n, job in enumerate(_ORDER)}
PER_T = 1 + len(_ORDER)
assert PER_T % 2 == 0 and len(F_EVAC) == TT and max(F_EVAC) < STEPS + 1


def ring(i, job):
    return PER_T * i + (TT - 1) + PLACE[job]


def slot(job):
    return (TT - 1 + PLACE[job]) % 2


def build(nc, x, gate, wq, bq, wk, bk, wv, bv, wo, bo, w1, b1, w2, b2, gamma1, beta1, gamma2, beta2, out):
    B = x.shape[0]
    x_rows = x.rearrange("b (t p) c -> b t p c", p=P)
    out_rows = out.rearrange("b (t p) c -> b t p c", p=P)

    def column(v):
        return v.rearrange("(c p) -> p c", p=P)

    def row(v):
        return v.rearrange("(a n) -> a n", a=1).to_broadcast([P, v.shape[0]])

    with ExitStack() as ctx:
        def sb(name, shape, dt=F32):
            return ctx.enter_context(nc.sbuf_tensor(name, shape, dt))

        def bank(name):
            return ctx.enter_context(nc.psum_tensor(name, [P, 512], F32))

        def sem(name):
            return ctx.enter_context(nc.semaphore(name))

        w_hi = sb("w_hi", [P, 4, DK, C], F16)
        w_lo = sb("w_lo", [P, 4, DK, C], F16)
        w1_hi, w1_lo = sb("w1_hi", [P, DK, FF], F16), sb("w1_lo", [P, DK, FF], F16)
        w2_hi, w2_lo = sb("w2_hi", [P, FJ, C], F16), sb("w2_lo", [P, FJ, C], F16)
        g_all = sb("g_all", [P, 2, FJ, T], F16)
        g_hi, g_lo = g_all[:, 0], g_all[:, 1]
        qk_parts = g_all[:].rearrange("p a j t -> p (a j) t")[:, 0:4 * DK, :].rearrange(
            "p (m s d) t -> p m s d t", m=2, s=2)
        w_stage = g_all[:].rearrange("p a j t -> p (a j t)").bitcast(F32)
        w1_stage = w_stage.rearrange("p (k n) -> p k n", k=DK)
        w2_stage = w_stage.rearrange("p (j c) -> p j c", j=FJ)
        stacks = sb("stacks", [P, 2, HPT, DK, T], F16)
        qkvo_stage = stacks[:].rearrange("p m j d t -> p (m j d t)").bitcast(F32).rearrange(
            "p (m k c) -> p m k c", m=4, k=DK)
        z_hi, z_lo = sb("z_hi", [P, DK, T], F16), sb("z_lo", [P, DK, T], F16)
        h2_hi, h2_lo = sb("h2_hi", [P, DK, T], F16), sb("h2_lo", [P, DK, T], F16)
        v_hi, v_lo = sb("v_hi", [P, TT, C], F16), sb("v_lo", [P, TT, C], F16)
        base = sb("base", [P, TT, C])
        probs = sb("probs", [P, 2, 512])
        pt_hi, pt_lo = sb("pt_hi", [P, 3, 512], F16), sb("pt_lo", [P, 3, 512], F16)
        ctx_rows = sb("ctx_rows", [P, C])
        ctx_hi, ctx_lo = sb("ctx_hi", [P, DK, P], F16), sb("ctx_lo", [P, DK, P], F16)
        att = sb("att", [P, C])
        xn = sb("xn", [P, 2, C])
        x1 = sb("x1", [P, C])
        out_sb = sb("out_sb", [P, C])
        bo_row, b2_row = sb("bo_row", [P, C]), sb("b2_row", [P, C])
        mask = sb("mask", [P, P], BF16)
        ident_b = sb("ident_b", [P, P], BF16)
        ident = sb("ident", [P, P])
        ones = out_sb[:, 0:P]
        bv_wide = att[:].rearrange("p (k n) -> p k n", k=DK)
        sums, rsums = sb("sums", [P, 2, NH]), sb("rsums", [P, NH])
        rmax, umax, nmax = sb("rmax", [P, 2, TT]), sb("umax", [P, 2, TT]), sb("nmax", [P, 2, TT])
        st6, mv = sb("st6", [P, 2, 6]), sb("mv", [P, 2, 2])
        veps, rstd = sb("veps", [P, 2]), sb("rstd", [P, 2])
        gates, gates_f = sb("gates", [P, B]), sb("gates_f", [P, B])
        gate_now, gate_before = sb("gate_now", [P, 1]), sb("gate_before", [P, 1])
        gam1, bet1 = sb("gam1", [P, DK]), sb("bet1", [P, DK])
        gam2, bet2 = sb("gam2", [P, DK]), sb("bet2", [P, DK])
        b_qkv, b_1 = sb("b_qkv", [P, 3, DK]), sb("b_1", [P, FJ])
        bs_qk = sb("bs_qk", [P, 2, DK])
        sq_w, sq_f = sb("sq_w", [P, 4, DK]), sb("sq_f", [P, 2, DK])
        sq_b, red = sb("sq_b", [P, FJ]), sb("red", [P, 2, TT])
        stat, pw, scale = sb("stat", [P, 6]), sb("pw", [P, 6]), sb("scale", [P, 6])
        c_half, c_eps = sb("c_half", [P, 6]), sb("c_eps", [P, 1])
        pad = sb("pad", [P, 1])
        gs = sb("gs", [P, 4, DK])
        exp_scale, exp_wide, log_p = sb("exp_scale", [P, 1]), sb("exp_wide", [P, TT]), sb("log_p", [P, TT])
        co, cf, inv_s1, prod = sb("co", [P, 1]), sb("cf", [P, 1]), sb("inv_s1", [P, 1]), sb("prod", [P, 3])

        score_ps = [bank("score0"), bank("score1")]
        trans_ps = [bank("trans0"), bank("trans1")]
        value_ps = [bank("value0"), bank("value1")]
        dense_ps = [bank("dense0"), bank("dense1")]

        cols_in, x_first = sem("cols_in"), sem("x_first")
        w_in = [sem(f"w_in{m}") for m in range(4)]
        w1_in, w2_in = sem("w1_in"), sem("w2_in")
        consts_made = sem("consts_made")
        squared = sem("squared")
        biased = sem("biased")
        stat_part = sem("stat_part")
        summed = sem("summed")
        stat_ready, powered = sem("stat_ready"), sem("powered")
        scaled = sem("scaled")
        chain = sem("chain")
        high_split, low_split = sem("high_split"), sem("low_split")
        bv_ready, bo_filled = sem("bv_ready"), sem("bo_filled")
        x_in = [sem("x_in0"), sem("x_in1")]
        res_in = [sem("res_in0"), sem("res_in1")]
        row_aux, row_stats = sem("row_aux"), sem("row_stats")
        row_veps, row_rstd = sem("row_veps"), sem("row_rstd")
        z_ready, h2_ready = sem("z_ready"), sem("h2_ready")
        t_filled, t_high, t_low = sem("t_filled"), sem("t_high"), sem("t_low")
        qkv_filled, qkv_high, qkv_low = sem("qkv_filled"), sem("qkv_high"), sem("qkv_low")
        stacked = sem("stacked")
        scored, maxed, shifted, neg_ready = sem("scored"), sem("maxed"), sem("shifted"), sem("neg_ready")
        exp_done, valued = sem("exp_done"), sem("valued")
        ctx_aux, ctx_ready = sem("ctx_aux"), sem("ctx_ready")
        wo_filled, att_ready = sem("wo_filled"), sem("att_ready")
        x1_ready, attb_ready, base_ready = sem("x1_ready"), sem("attb_ready"), sem("base_ready")
        gate_set = sem("gate_set")
        f1_filled, gelu_done, g_high, g_low = sem("f1_filled"), sem("gelu_done"), sem("g_high"), sem("g_low")
        f2_filled, out_ready, stored = sem("f2_filled"), sem("out_ready"), sem("stored")

        block = ctx.enter_context(nc.Block())
        STACK_DMAS = 2 * PARTS * HPT
        QKV = 3 * DK
        SPLITS = 3 * DK + 1

        @block.sync
        def _(sp):
            def stack_parts(i):
                for m, kinds in enumerate(((0, 0, 1), (0, 1, 0))):
                    sp.wait_ge(qkv_low, QKV * i + DK * (m + 1))
                    for part, kind in enumerate(kinds):
                        for j in range(HPT):
                            sp.dma_start(stacks[DH * part:DH * (part + 1), m, j],
                                         qk_parts[DH * j:DH * (j + 1), m, kind]).then_inc(stacked, 16)

            def load_x(i, nxt, t):
                before = ring(i, ("z", t - 2)) if t >= 2 else ring(i - 1, ("z", t + 2))
                sp.wait_ge(t_filled, before + 1)
                sp.dma_start(xn[:, t % 2], x_rows[nxt, t]).then_inc(x_in[t % 2], 16)

            def store_out(f, t):
                sp.wait_ge(out_ready, TT * f + t + 2)
                sp.dma_start(out_rows[f, t], out_sb[:]).then_inc(stored, 16)

            def iteration(i, nxt):
                stack_parts(i)
                load_x(i, nxt, 0)
                load_x(i, nxt, 1)
                for t in range(TT):
                    store_out(i - 1, t)
                    sp.dma_start(base[:, t], x_rows[i, t]).then_inc(res_in[t % 2], 16)
                    if t < 2:
                        load_x(i, nxt, t + 2)

            for m, w in enumerate((wq, wk, wv, wo)):
                sp.dma_start(qkvo_stage[:, m], w.rearrange("(k p) c -> p k c", p=P)).then_inc(w_in[m], 16)
            stack_parts(0)
            for t in range(2):
                sp.wait_ge(t_filled, t + 3)
                sp.dma_start(xn[:, t], x_rows[1, t]).then_inc(x_in[t], 16)
            sp.wait_ge(stacked, 16 * STACK_DMAS)
            sp.dma_start(w1_stage, w1.rearrange("(k p) n -> p k n", p=P)).then_inc(w1_in, 16)
            load_x(0, 1, 2)
            sp.wait_ge(low_split, SPLITS + DK)
            sp.dma_start(w2_stage, w2.rearrange("(j p) c -> p j c", p=P)).then_inc(w2_in, 16)
            load_x(0, 1, 3)
            with sp.Fori(1, B - 1) as i:
                iteration(i, i + 1)
            iteration(B - 1, B - 1)
            for t in range(TT):
                store_out(B - 1, t)
            sp.wait_ge(stored, 16 * TT * B)

        @block.gpsimd
        def _(pool):
            pool.memset(c_half[:], -0.5).then_inc(consts_made, 1)
            pool.memset(c_eps[:], EPS).then_inc(consts_made, 1)
            pool.memset(ones, 1.0).then_inc(consts_made, 1)
            pool.memset(ident[:], 0.0).then_inc(consts_made, 1)
            pool.memset(mask[:], 0.0).then_inc(consts_made, 1)
            pool.memset(ident_b[:], 0.0).then_inc(consts_made, 1)
            pool.wait_ge(consts_made, 6)
            pool.affine_select(out=ident_b[:], in_=ident_b[:], compare_op=ALU.not_equal, fill=1.0, base=0,
                               pattern=[[-1, P]], channel_multiplier=1).then_inc(consts_made, 1)
            pool.affine_select(out=ident[:], in_=ident[:], compare_op=ALU.not_equal, fill=1.0, base=0,
                               pattern=[[-1, P]], channel_multiplier=1).then_inc(consts_made, 1)
            pool.affine_select(out=mask[:], in_=mask[:], compare_op=ALU.is_ge, fill=MASKED, base=0,
                               pattern=[[-1, P]], channel_multiplier=1).then_inc(consts_made, 1)

            def inverse_std(n, which):
                pool.wait_ge(row_stats, n)
                pool.tensor_tensor(veps[:, which:which + 1], mv[:, which, 1:2], c_eps[:],
                                   ALU.add).then_inc(row_veps, 1)
                pool.wait_ge(row_veps, n)
                pool.tensor_tensor(rstd[:, which:which + 1], veps[:, which:which + 1], c_half[:, 0:1],
                                   ALU.pow).then_inc(row_rstd, 1)

            def residual(i, t, first):
                pool.wait_ge(att_ready, TT * i + t + 1)
                if not first:
                    pool.wait_ge(res_in[t % 2], 16 * (TT // 2 * (i - 1) + t // 2 + 1))
                pool.tensor_tensor(x1[:], base[:, t], att[:], ALU.add).then_inc(x1_ready, 1)
                pool.wait_ge(x1_ready, TT * i + t + 1)
                pool.tensor_tensor(att[:], att[:], b2_row[:], ALU.add).then_inc(attb_ready, 1)

            def negate(i, g):
                heads = GROUPS[g][2]
                pool.wait_ge(maxed, NG * i + g + 1)
                pool.tensor_tensor(umax[:, g % 2, 0:heads], log_p[:, 0:heads], rmax[:, g % 2, 0:heads],
                                   ALU.subtract).then_inc(shifted, 1)
                pool.wait_ge(shifted, NG * i + g + 1)
                pool.tensor_tensor(nmax[:, g % 2, 0:heads], umax[:, g % 2, 0:heads], exp_wide[:, 0:heads],
                                   ALU.mult).then_inc(neg_ready, 1)

            def attention(i, first):
                n = TT + 2 * TT * i
                if first:
                    pool.wait_ge(scaled, 1)
                negate(i, 0)
                for s in range(STEPS):
                    if s + 1 < NG:
                        negate(i, s + 1)
                    if first and s in (SETUP_1 + 2, SETUP_2 + 5):
                        k = 4 if s == SETUP_1 + 2 else 5
                        pool.wait_ge(stat_ready, k - 2)
                        pool.tensor_tensor(pw[:, k:k + 1], stat[:, k:k + 1], c_half[:, 0:1],
                                           ALU.pow).then_inc(powered, 1)
                    if s in W_EVAC:
                        residual(i, W_EVAC[s], first)
                    for kind, t in ROWS_AT[s]:
                        n = n + 1
                        inverse_std(n, int(kind == "h2"))
                residual(i, TT - 1, first)
                inverse_std(n + 1, 1)

            for t in range(TT):
                inverse_std(t + 1, 0)
            pool.wait_ge(stat_ready, 1)
            pool.tensor_tensor(pw[:, 0:4], stat[:, 0:4], c_half[:, 0:4], ALU.pow).then_inc(powered, 1)
            attention(0, True)
            with pool.Fori(1, B) as i:
                attention(i, False)

        @block.scalar
        def _(act):
            def high(i, job):
                kind, n = job
                act.wait_ge(t_filled, ring(i, job) + 1)
                high_of(kind, n, slot(job))

            def high_of(kind, n, b):
                if kind == "p":
                    width = GROUPS[n][2] * (GROUPS[n][0] + 1) * P
                    act.activation(pt_hi[:, n % 3, 0:width], trans_ps[b][:, 0:width], ACT.Copy).then_inc(t_high, 1)
                    return
                dst = {"ctx": ctx_hi, "z": z_hi, "h2": h2_hi}[kind]
                dst = dst[:] if kind == "ctx" else dst[:, :, n * P:(n + 1) * P]
                act.activation(dst, trans_ps[b][:].rearrange("p (k t) -> p k t", k=DK), ACT.Copy).then_inc(t_high, 1)

            def project(i, first):
                for j in range(QKV):
                    m, n = j // DK, j % DK
                    act.wait_ge(qkv_filled, QKV * i + j + 1)
                    if m < 2:
                        act.activation(qk_parts[:, m, 0, n], dense_ps[j % 2][:], ACT.Identity,
                                       bias=bs_qk[:, m, n:n + 1]).then_inc(qkv_high, 1)
                    else:
                        act.activation(v_hi[:, n], dense_ps[j % 2][:], ACT.Copy).then_inc(qkv_high, 1)
                    if j == H2_AT and not first:
                        high(i, ("h2", TT - 1))

            def feed_1(f):
                for j in range(FJ):
                    act.wait_ge(f1_filled, FJ * f + j + 1)
                    if j >= 2:
                        act.wait_ge(g_low, FJ * f + j - 1)
                    act.activation(probs[:, j % 2], dense_ps[j % 2][:], ACT.Gelu, bias=b_1[:, j:j + 1],
                                   scale=inv_s1[:]).then_inc(gelu_done, 1)

            def exps(i, g, first):
                qt, h0, heads = GROUPS[g]
                width = (qt + 1) * P
                act.wait_ge(neg_ready, NG * i + g + 1)
                if g < 2 and not first:
                    act.wait_ge(g_low, FJ * i)
                if g == FIRST[qt] and (qt >= 2 or not first):
                    act.wait_ge(ctx_ready, TT * i + qt - 1)
                for a in range(heads):
                    e = act.activation(probs[:, g % 2, a * width:(a + 1) * width],
                                       score_ps[g % 2][:, a * width:(a + 1) * width], ACT.Exp,
                                       bias=nmax[:, g % 2, a:a + 1], scale=exp_scale[:],
                                       accum_out=sums[:, qt % 2, h0 + a:h0 + a + 1])
                e.then_inc(exp_done, 1)

            def attention(i, first):
                for s in range(STEPS):
                    if s < NG:
                        exps(i, s, first)
                    if 1 <= s <= NG:
                        high(i, ("p", s - 1))
                    for job in OTHERS[s]:
                        high(i, job)
                    if first:
                        if s == SETUP_1:
                            act.wait_ge(w1_in, 16)
                            for k in range(DK):
                                act.activation(w1_hi[:, k], w1_stage[:, k], ACT.Square, scale=gam2[:, k:k + 1],
                                               accum_out=sq_f[:, 0, k:k + 1]).then_inc(squared, 1)
                        if SETUP_1 + 3 <= s < SETUP_1 + 3 + DK:
                            k = s - SETUP_1 - 3
                            act.wait_ge(scaled, 2)
                            act.activation(w1_hi[:, k], w1_stage[:, k], ACT.Copy,
                                           scale=gs[:, 3, k:k + 1]).then_inc(high_split, 1)
                        if SETUP_2 <= s < SETUP_2 + DK:
                            k = s - SETUP_2
                            act.wait_ge(w2_in, 16)
                            act.activation(w2_hi[:, 4 * k:4 * k + 4], w2_stage[:, 4 * k:4 * k + 4], ACT.Square,
                                           accum_out=sq_f[:, 1, k:k + 1]).then_inc(squared, 1)
                        if SETUP_2 + 6 <= s < SETUP_2 + 6 + DK:
                            k = s - SETUP_2 - 6
                            act.wait_ge(scaled, 3)
                            act.activation(w2_hi[:, 4 * k:4 * k + 4], w2_stage[:, 4 * k:4 * k + 4], ACT.Copy,
                                           scale=scale[:, 5:6]).then_inc(high_split, 1)

            for t in range(0, TT, 2):
                act.dma_start(base[:, t:t + 2], x_rows[0].rearrange("t p c -> p t c")[:, t:t + 2]).then_inc(x_first, 16)
            for tile, v in ((gam1, gamma1), (bet1, beta1), (gam2, gamma2), (bet2, beta2), (b_1, b1)):
                act.dma_start(tile[:], column(v), allow_slow_non_contiguous=True).then_inc(cols_in, 16)
            for m, v in enumerate((bq, bk, bv)):
                act.dma_start(b_qkv[:, m], column(v), allow_slow_non_contiguous=True).then_inc(cols_in, 16)
            act.dma_start(bo_row[:], row(bo)).then_inc(cols_in, 16)
            act.dma_start(b2_row[:], row(b2)).then_inc(cols_in, 16)
            act.dma_start(gates[:], row(gate)).then_inc(cols_in, 16)
            for t in range(TT):
                act.wait_ge(t_filled, t + 1)
                high_of("z", t, t % 2)
            act.wait_ge(cols_in, 16 * COLS)
            for m in range(3):
                act.wait_ge(w_in[m], 16)
                for k in range(DK):
                    act.activation(w_hi[:, m, k], qkvo_stage[:, m, k], ACT.Square, scale=gam1[:, k:k + 1],
                                   accum_out=sq_w[:, m, k:k + 1]).then_inc(squared, 1)
            act.wait_ge(w_in[3], 16)
            act.activation(w_hi[:, 3], qkvo_stage[:, 3], ACT.Square,
                           accum_out=sq_w[:, 3, 0:1]).then_inc(squared, 1)
            act.wait_ge(scaled, 1)
            for m in range(3):
                for k in range(DK):
                    act.activation(w_hi[:, m, k], qkvo_stage[:, m, k], ACT.Copy,
                                   scale=gs[:, m, k:k + 1]).then_inc(high_split, 1)
            act.activation(w_hi[:, 3], qkvo_stage[:, 3], ACT.Copy, scale=scale[:, 3:4]).then_inc(high_split, 1)
            project(0, True)
            attention(0, True)
            with act.Fori(1, B) as i:
                project(i, False)
                feed_1(i - 1)
                attention(i, False)
            high(B, ("h2", TT - 1))
            feed_1(B - 1)

        @block.tensor
        def _(pe):
            def turn(i, job):
                kind, n = job
                pe.wait_ge(t_low, ring(i, job) - 1)
                if kind == "p":
                    pe.wait_ge(exp_done, NG * i + n + 1)
                    src = [probs[:, n % 2, b * P:(b + 1) * P] for b in range(GROUPS[n][2] * (GROUPS[n][0] + 1))]
                elif kind == "ctx":
                    pe.wait_ge(ctx_ready, TT * i + n + 1)
                    src = [ctx_rows[:, k * P:(k + 1) * P] for k in range(DK)]
                elif kind == "z":
                    pe.wait_ge(z_ready, TT * (i + 1) + n + 1)
                    src = [xn[:, n % 2, k * P:(k + 1) * P] for k in range(DK)]
                else:
                    pe.wait_ge(h2_ready, TT * (i - (n == TT - 1)) + n + 1)
                    src = [x1[:, k * P:(k + 1) * P] for k in range(DK)]
                for b, block_in in enumerate(src):
                    last = pe.transpose(trans_ps[slot(job)][:, b * P:(b + 1) * P], block_in, ident[:])
                last.then_inc(t_filled, 1)

            def project(i, first):
                pe.wait_ge(t_low, TT if first else ring(i - 1, ("z", TT - 1)) + 1)
                for j in range(QKV):
                    m, n = j // DK, j % DK
                    ps = dense_ps[j % 2]
                    if j >= 2:
                        pe.wait_ge(qkv_low, QKV * i + j - 1)
                    elif j == 1 and not first:
                        pe.wait_ge(att_ready, TT * i)
                    elif not first:
                        pe.wait_ge(out_ready, TT * i - TT + 1)
                    for k in range(DK):
                        for ws, zs in ((w_hi, z_hi), (w_hi, z_lo), (w_lo, z_hi)):
                            if m < 2:
                                a, b = ws[:, m, k, n * P:(n + 1) * P], zs[:, k]
                            else:
                                a, b = zs[:, k, n * P:(n + 1) * P], ws[:, m, k]
                            last = pe.matmul(ps[:], a, b, start=(k == 0 and ws is w_hi and zs is z_hi),
                                             stop=(k == DK - 1 and ws is w_lo))
                    last.then_inc(qkv_filled, 1)
                    if j == H2_AT and not first:
                        turn(i, ("h2", TT - 1))

            def feed_1(f, last_item=False):
                pe.wait_ge(t_low, ring(f + 1, ("h2", TT - 1)) + 1)
                for j in range(FJ):
                    ps = dense_ps[j % 2]
                    if j >= 2:
                        pe.wait_ge(gelu_done, FJ * f + j - 1)
                    elif not last_item:
                        pe.wait_ge(qkv_low, QKV * (f + 2) - 1 + j)
                    elif j == 0:
                        pe.wait_ge(out_ready, TT * f + 1)
                    else:
                        pe.wait_ge(att_ready, TT * (f + 1))
                    for k in range(DK):
                        for n, (ws, hs) in enumerate(((w1_hi, h2_hi), (w1_hi, h2_lo), (w1_lo, h2_hi))):
                            last = pe.matmul(ps[:], ws[:, k, j * P:(j + 1) * P], hs[:, k],
                                             start=(k == 0 and n == 0), stop=(k == DK - 1 and n == 2))
                    last.then_inc(f1_filled, 1)

            def feed_2(f, t, n):
                if n == 0 and t == 0:
                    pe.wait_ge(g_low, FJ * (f + 1))
                elif n == 0:
                    pe.wait_ge(out_ready, TT * f + t + 1)
                j = n // 3
                gsrc, wsrc = ((g_hi, w2_hi), (g_hi, w2_lo), (g_lo, w2_hi))[n % 3]
                mm = pe.matmul(dense_ps[0][:], gsrc[:, j, t * P:(t + 1) * P], wsrc[:, j],
                               start=(n == 0), stop=(n == F_MMS - 1))
                if n == F_MMS - 1:
                    mm.then_inc(f2_filled, 1)

            def output(i, t, n, first):
                if n == 0:
                    pe.wait_ge(t_low, ring(i, ("ctx", t)) + 1)
                    if t > 0:
                        pe.wait_ge(att_ready, TT * i + t)
                    elif first:
                        pe.wait_ge(qkv_low, QKV)
                    else:
                        pe.wait_ge(gelu_done, FJ * i)
                k = n // 3
                csrc, wsrc = ((ctx_hi, w_hi), (ctx_hi, w_lo), (ctx_lo, w_hi))[n % 3]
                mm = pe.matmul(dense_ps[1][:], csrc[:, k], wsrc[:, 3, k], start=(n == 0), stop=(n == W_MMS - 1))
                if n == W_MMS - 1:
                    mm.then_inc(wo_filled, 1)

            def dense(i, first, jobs):
                for kind, t, n in jobs:
                    if kind == "W":
                        output(i, t, n, first)
                    elif not first:
                        feed_2(i - 1, t, n)

            def scores(i, g, first):
                qt, h0, heads = GROUPS[g]
                width = (qt + 1) * P
                if g == 0:
                    pe.wait_ge(stacked, 16 * STACK_DMAS * (i + 1))
                if g >= 2 or not first:
                    pe.wait_ge(exp_done, NG * i + g - 1)
                for a in range(heads):
                    dt, j = divmod(h0 + a, HPT)
                    pe.matmul(score_ps[g % 2][:, a * width:(a + 1) * width],
                              stacks[0:PARTS * DH, 0, j, dt, qt * P:(qt + 1) * P],
                              stacks[0:PARTS * DH, 1, j, dt, 0:width], start=True, stop=False,
                              skip_group_check=True)
                    last = pe.matmul(score_ps[g % 2][:, a * width + qt * P:(a + 1) * width], ident_b[:], mask[:],
                                     start=False, stop=True, skip_group_check=True)
                last.then_inc(scored, 1)

            def values(i, g, first):
                qt, h0, heads = GROUPS[g]
                pe.wait_ge(t_low, ring(i, ("p", g)) + 1)
                if g == FIRST[qt] and (qt >= 2 or not first):
                    pe.wait_ge(ctx_ready, TT * i + qt - 1)
                for a in range(heads):
                    cols = slice((h0 + a) * DH, (h0 + a + 1) * DH)
                    for kt in range(qt + 1):
                        b = slice((a * (qt + 1) + kt) * P, (a * (qt + 1) + kt + 1) * P)
                        for n, (ps, vs) in enumerate(((pt_hi, v_hi), (pt_hi, v_lo), (pt_lo, v_hi))):
                            last = pe.matmul(value_ps[qt % 2][:, cols], ps[:, g % 3, b], vs[:, kt, cols],
                                             start=(g == FIRST[qt] and a == 0 and kt == 0 and n == 0),
                                             stop=(g == LAST[qt] and a == heads - 1 and kt == qt and n == 2),
                                             skip_group_check=True)
                if g == LAST[qt]:
                    last.then_inc(valued, 1)

            def ff_setup(s):
                if s == SETUP_1:
                    pe.wait_ge(w1_in, 16)
                    for j in range(FJ):
                        for k in range(DK):
                            last = pe.matmul(dense_ps[0][:, j:j + 1], w1_stage[:, k, j * P:(j + 1) * P],
                                             bet2[:, k:k + 1], start=(k == 0), stop=(k == DK - 1))
                    last.then_inc(biased, 1)
                if s in (SETUP_1 + 2, SETUP_2 + 5):
                    k = 4 if s == SETUP_1 + 2 else 5
                    pe.wait_ge(stat_part, k - 2)
                    pe.matmul(dense_ps[0][:, k:k + 1], ones, stat[:, k:k + 1], start=True,
                              stop=True).then_inc(summed, 1)

            def attention(i, first):
                scores(i, 0, first)
                for s in range(STEPS):
                    jobs = DENSE[CUT[s]:CUT[s + 1]]
                    half = (len(jobs) + 1) // 2
                    if s + 1 < NG:
                        scores(i, s + 1, first)
                    if 1 <= s <= NG:
                        turn(i, ("p", s - 1))
                    dense(i, first, jobs[:half])
                    for job in OTHERS[s]:
                        turn(i, job)
                    dense(i, first, jobs[half:])
                    if 3 <= s < NG + 3:
                        values(i, s - 3, first)
                    if first:
                        ff_setup(s)
                for n in range(W_MMS):
                    output(i, TT - 1, n, first)

            pe.wait_ge(consts_made, CONSTS)
            for t in range(TT):
                pe.wait_ge(z_ready, t + 1)
                if t >= 2:
                    pe.wait_ge(t_low, t - 1)
                for k in range(DK):
                    last = pe.transpose(trans_ps[t % 2][:, k * P:(k + 1) * P], xn[:, t % 2, k * P:(k + 1) * P],
                                        ident[:])
                last.then_inc(t_filled, 1)
            pe.wait_ge(cols_in, 16 * COLS)
            for m in range(3):
                pe.wait_ge(w_in[m], 16)
                for n in range(DK):
                    for k in range(DK):
                        last = pe.matmul(dense_ps[0][:, m * DK + n:m * DK + n + 1],
                                         qkvo_stage[:, m, k, n * P:(n + 1) * P], bet1[:, k:k + 1],
                                         start=(k == 0), stop=(k == DK - 1))
            last.then_inc(biased, 1)
            pe.wait_ge(stat_part, 1)
            pe.matmul(dense_ps[1][:, 0:4], ones, stat[:, 0:4], start=True, stop=True).then_inc(summed, 1)
            pe.wait_ge(bv_ready, DK)
            pe.wait_ge(w_in[3], 16)
            for k in range(DK):
                last = pe.matmul(dense_ps[0][:], bv_wide[:, k], qkvo_stage[:, 3, k], start=(k == 0),
                                 stop=(k == DK - 1))
            last.then_inc(bo_filled, 1)
            pe.wait_ge(low_split, SPLITS)
            project(0, True)
            attention(0, True)
            with pe.Fori(1, B) as i:
                project(i, False)
                feed_1(i - 1)
                attention(i, False)
            turn(B, ("h2", TT - 1))
            feed_1(B - 1, last_item=True)
            for t in range(TT):
                for n in range(F_MMS):
                    feed_2(B - 1, t, n)

        @block.vector
        def _(dve):
            steps = [0]

            def link(ins):
                steps[0] += 1
                ins.then_inc(chain, 1)
                dve.wait_ge(chain, steps[0])

            def low_of(kind, n, b):
                if kind == "p":
                    width = GROUPS[n][2] * (GROUPS[n][0] + 1) * P
                    dve.tensor_tensor(pt_lo[:, n % 3, 0:width], trans_ps[b][:, 0:width],
                                      pt_hi[:, n % 3, 0:width], ALU.subtract).then_inc(t_low, 1)
                    return
                hi, lo = {"ctx": (ctx_hi, ctx_lo), "z": (z_hi, z_lo), "h2": (h2_hi, h2_lo)}[kind]
                cols = slice(0, P) if kind == "ctx" else slice(n * P, (n + 1) * P)
                dve.tensor_tensor(lo[:, :, cols], trans_ps[b][:].rearrange("p (k t) -> p k t", k=DK),
                                  hi[:, :, cols], ALU.subtract).then_inc(t_low, 1)

            def low(i, job):
                dve.wait_ge(t_high, ring(i, job) + 1)
                low_of(*job, slot(job))

            def row_statistics(n, which, rows):
                dve.bn_stats(st6[:, which], rows).then_inc(row_aux, 1)
                dve.wait_ge(row_aux, n)
                dve.memset(pad[:], 0.0)
                dve.bn_aggr(mv[:, which], st6[:, which]).then_inc(row_stats, 1)

            def norm(n, which, dst, rows, ready):
                dve.wait_ge(row_rstd, n)
                dve.tensor_scalar(dst, rows, mv[:, which, 0:1], rstd[:, which:which + 1], ALU.subtract,
                                  ALU.mult).then_inc(ready, 1)

            def project(i, first):
                for j in range(QKV):
                    m, n = j // DK, j % DK
                    dve.wait_ge(qkv_high, QKV * i + j + 1)
                    if m < 2:
                        dve.scalar_tensor_tensor(qk_parts[:, m, 1, n], dense_ps[j % 2][:], bs_qk[:, m, n:n + 1],
                                                 qk_parts[:, m, 0, n], ALU.add, ALU.subtract).then_inc(qkv_low, 1)
                    else:
                        dve.tensor_tensor(v_lo[:, n], dense_ps[j % 2][:], v_hi[:, n],
                                          ALU.subtract).then_inc(qkv_low, 1)
                    if j == H2_AT and not first:
                        low(i, ("h2", TT - 1))

            def feed_1(f, last_item=False):
                for j in range(FJ):
                    dve.wait_ge(gelu_done, FJ * f + j + 1)
                    if j == 0 and not last_item:
                        dve.wait_ge(stacked, 16 * STACK_DMAS * (f + 2))
                    dve.tensor_scalar(g_hi[:, j], probs[:, j % 2], scale[:, 4:5], None,
                                      ALU.mult).then_inc(g_high, 1)
                    dve.wait_ge(g_high, FJ * f + j + 1)
                    dve.scalar_tensor_tensor(g_lo[:, j], probs[:, j % 2], scale[:, 4:5], g_hi[:, j],
                                             ALU.mult, ALU.subtract).then_inc(g_low, 1)

            def maxima(i, g):
                qt, h0, heads = GROUPS[g]
                width = (qt + 1) * P
                ps = score_ps[g % 2][:, 0:heads * width].rearrange("p (a k) -> p a k", a=heads)
                dve.wait_ge(scored, NG * i + g + 1)
                dve.tensor_reduce(rmax[:, g % 2, 0:heads], ps, AX_X, ALU.max).then_inc(maxed, 1)

            def context(i, qt):
                dve.wait_ge(valued, TT * i + qt + 1)
                dve.wait_ge(exp_done, NG * i + LAST[qt] + 1)
                dve.reciprocal(rsums[:], sums[:, qt % 2]).then_inc(ctx_aux, 1)
                dve.wait_ge(ctx_aux, TT * i + qt + 1)
                dve.tensor_tensor(ctx_rows[:].rearrange("p (h d) -> p h d", h=NH),
                                  value_ps[qt % 2][:].rearrange("p (h d) -> p h d", h=NH),
                                  rsums[:].unsqueeze(2).to_broadcast([P, NH, DH]), ALU.mult).then_inc(ctx_ready, 1)

            def attention_rows(i, t):
                dve.wait_ge(wo_filled, TT * i + t + 1)
                dve.scalar_tensor_tensor(att[:], dense_ps[1][:], co[:], bo_row[:], ALU.mult,
                                         ALU.add).then_inc(att_ready, 1)

            def base_rows(i, t):
                dve.wait_ge(attb_ready, TT * i + t + 1)
                dve.scalar_tensor_tensor(base[:, t], att[:], gate_now[:], base[:, t], ALU.mult,
                                         ALU.add).then_inc(base_ready, 1)

            def output_rows(f, t):
                dve.wait_ge(f2_filled, TT * f + t + 1)
                dve.wait_ge(base_ready, TT * (f + 1))
                if t:
                    dve.wait_ge(stored, 16 * (TT * f + t))
                dve.scalar_tensor_tensor(out_sb[:], dense_ps[0][:], gate_before[:], base[:, t], ALU.mult,
                                         ALU.add).then_inc(out_ready, 1)

            def ff_setup(s):
                if s == SETUP_1 + 1:
                    dve.wait_ge(biased, 2)
                    link(dve.tensor_tensor(b_1[:], b_1[:], dense_ps[0][:, 0:FJ], ALU.add))
                    link(dve.tensor_tensor(sq_b[:], b_1[:], b_1[:], ALU.mult))
                    link(dve.tensor_reduce(red[:, 0, 0:1], sq_b[:], AX_X, ALU.add))
                    dve.wait_ge(squared, SPLITS + DK)
                    link(dve.tensor_reduce(red[:, 1, 0:1], sq_f[:, 0], AX_X, ALU.add))
                    dve.scalar_tensor_tensor(stat[:, 4:5], red[:, 0, 0:1], 1.0 / C, red[:, 1, 0:1], ALU.mult,
                                             ALU.add).then_inc(stat_part, 1)
                if s == SETUP_2 + 4:
                    dve.wait_ge(squared, SPLITS + 2 * DK)
                    dve.tensor_reduce(stat[:, 5:6], sq_f[:, 1], AX_X, ALU.add).then_inc(stat_part, 1)
                if s in (SETUP_1 + 2, SETUP_2 + 5):
                    k = 4 if s == SETUP_1 + 2 else 5
                    dve.wait_ge(summed, k - 2)
                    dve.tensor_scalar(stat[:, k:k + 1], dense_ps[0][:, k:k + 1], TINY, None,
                                      ALU.add).then_inc(stat_ready, 1)
                    dve.wait_ge(powered, k - 2)
                    link(dve.tensor_scalar(scale[:, k:k + 1], pw[:, k:k + 1], NORM_TO, None, ALU.mult))
                    if k == 4:
                        link(dve.reciprocal(inv_s1[:], scale[:, 4:5]))
                        dve.tensor_scalar(gs[:, 3], gam2[:], scale[:, 4:5], None, ALU.mult).then_inc(scaled, 1)
                    else:
                        link(dve.tensor_tensor(prod[:, 2:3], scale[:, 4:5], scale[:, 5:6], ALU.mult))
                        dve.reciprocal(cf[:], prod[:, 2:3]).then_inc(out_ready, 1)
                        dve.wait_ge(out_ready, 1)
                        dve.tensor_scalar(gates_f[:], gates[:], cf[:], None, ALU.mult).then_inc(scaled, 1)

                if SETUP_1 + 3 <= s < SETUP_1 + 3 + DK:
                    k = s - SETUP_1 - 3
                    dve.wait_ge(high_split, SPLITS + k + 1)
                    dve.scalar_tensor_tensor(w1_lo[:, k], w1_stage[:, k], gs[:, 3, k:k + 1], w1_hi[:, k],
                                             ALU.mult, ALU.subtract).then_inc(low_split, 1)
                if SETUP_2 + 6 <= s < SETUP_2 + 6 + DK:
                    k = s - SETUP_2 - 6
                    dve.wait_ge(high_split, SPLITS + DK + k + 1)
                    rows = slice(4 * k, 4 * k + 4)
                    dve.scalar_tensor_tensor(w2_lo[:, rows], w2_stage[:, rows], scale[:, 5:6], w2_hi[:, rows],
                                             ALU.mult, ALU.subtract).then_inc(low_split, 1)

            def attention(i, first):
                n = TT + 2 * TT * i
                taken = {}
                maxima(i, 0)
                for s in range(STEPS):
                    lows = [("p", s - 2)] * (2 <= s <= NG + 1) + OTHERS[s - 1] * (s > 0)
                    if s + 1 < NG and len(lows) == 1:
                        maxima(i, s + 1)
                    for job in lows:
                        low(i, job)
                    if s + 1 < NG and len(lows) != 1:
                        maxima(i, s + 1)
                    if s in CTX_EVAC:
                        context(i, CTX_EVAC[s])
                    if s in F_EVAC and not first:
                        output_rows(i - 1, F_EVAC[s])
                    if s in W_EVAC:
                        attention_rows(i, W_EVAC[s])
                    for kind, t in ROWS_AT[s]:
                        n = n + 1
                        taken[kind, t] = n
                        if kind == "h2":
                            dve.wait_ge(x1_ready, TT * i + t + 1)
                            row_statistics(n, 1, x1[:])
                        else:
                            dve.wait_ge(x_in[t % 2], 16 * (TT // 2 * i + t // 2 + 1))
                            row_statistics(n, 0, xn[:, t % 2])
                    if s - 2 in W_EVAC:
                        t = W_EVAC[s - 2]
                        norm(taken["h2", t], 1, x1[:], x1[:], h2_ready)
                        base_rows(i, t)
                    if s + 1 in Z_T:
                        t = Z_T[s + 1]
                        norm(taken["z", t], 0, xn[:, t % 2], xn[:, t % 2], z_ready)
                    if first:
                        ff_setup(s)
                for job in OTHERS[STEPS - 1]:
                    low(i, job)
                if STEPS in F_EVAC and not first:
                    output_rows(i - 1, F_EVAC[STEPS])
                attention_rows(i, TT - 1)
                dve.wait_ge(x1_ready, TT * (i + 1))
                row_statistics(n + 1, 1, x1[:])
                base_rows(i, TT - 1)
                norm(n + 1, 1, x1[:], x1[:], h2_ready)
                if not first:
                    dve.wait_ge(stored, 16 * TT * i)

            for t in range(TT):
                dve.wait_ge(x_first, 32)
                row_statistics(t + 1, 0, base[:, t])
                if t >= 2:
                    dve.wait_ge(t_filled, t - 1)
                norm(t + 1, 0, xn[:, t % 2], base[:, t], z_ready)
                if t >= 1:
                    dve.wait_ge(t_high, t)
                    low_of("z", t - 1, (t - 1) % 2)
            dve.wait_ge(t_high, TT)
            low_of("z", TT - 1, (TT - 1) % 2)
            dve.wait_ge(consts_made, CONSTS)
            dve.wait_ge(cols_in, 16 * COLS)
            dve.wait_ge(biased, 1)
            link(dve.tensor_tensor(b_qkv[:].rearrange("p m k -> p (m k)"), b_qkv[:].rearrange("p m k -> p (m k)"),
                                   dense_ps[0][:, 0:3 * DK], ALU.add))
            for k in range(DK):
                dve.tensor_copy(bv_wide[:, k], b_qkv[:, 2, k:k + 1].to_broadcast([P, P])).then_inc(bv_ready, 1)
            link(dve.tensor_tensor(sq_b[:, 0:3 * DK], b_qkv[:].rearrange("p m k -> p (m k)"),
                                   b_qkv[:].rearrange("p m k -> p (m k)"), ALU.mult))
            link(dve.tensor_reduce(red[:, 0, 0:3], sq_b[:, 0:3 * DK].rearrange("p (m k) -> p m k", m=3), AX_X, ALU.add))
            dve.wait_ge(squared, SPLITS)
            link(dve.tensor_reduce(red[:, 1, 0:3], sq_w[:, 0:3], AX_X, ALU.add))
            link(dve.tensor_copy(stat[:, 3:4], sq_w[:, 3, 0:1]))
            dve.scalar_tensor_tensor(stat[:, 0:3], red[:, 0, 0:3], 1.0 / C, red[:, 1, 0:3], ALU.mult,
                                     ALU.add).then_inc(stat_part, 1)
            dve.wait_ge(summed, 1)
            dve.tensor_scalar(stat[:, 0:4], dense_ps[1][:, 0:4], TINY, None, ALU.add).then_inc(stat_ready, 1)
            dve.wait_ge(powered, 1)
            link(dve.tensor_scalar(scale[:, 0:4], pw[:, 0:4], NORM_TO, None, ALU.mult))
            for m in range(3):
                link(dve.tensor_scalar(gs[:, m], gam1[:], scale[:, m:m + 1], None, ALU.mult))
            for m in range(2):
                link(dve.tensor_scalar(bs_qk[:, m], b_qkv[:, m], scale[:, m:m + 1], None, ALU.mult))
            link(dve.scalar_tensor_tensor(prod[:, 0:1], scale[:, 0:1], float(DH) ** 0.5, scale[:, 1:2],
                                          ALU.mult, ALU.mult))
            link(dve.tensor_tensor(prod[:, 1:2], scale[:, 2:3], scale[:, 3:4], ALU.mult))
            link(dve.reciprocal(exp_scale[:], prod[:, 0:1]))
            link(dve.reciprocal(co[:], prod[:, 1:2]))
            link(dve.tensor_copy(exp_wide[:], exp_scale[:].to_broadcast([P, TT])))
            dve.tensor_scalar(log_p[:], prod[:, 0:1].to_broadcast([P, TT]), LOG_P, None, ALU.mult).then_inc(scaled, 1)
            dve.wait_ge(bo_filled, 1)
            link(dve.tensor_tensor(bo_row[:], bo_row[:], dense_ps[0][:], ALU.add))
            for m in range(3):
                for k in range(DK):
                    dve.wait_ge(high_split, m * DK + k + 1)
                    dve.scalar_tensor_tensor(w_lo[:, m, k], qkvo_stage[:, m, k], gs[:, m, k:k + 1], w_hi[:, m, k],
                                             ALU.mult, ALU.subtract).then_inc(low_split, 1)
            dve.wait_ge(high_split, SPLITS)
            dve.scalar_tensor_tensor(w_lo[:, 3], qkvo_stage[:, 3], scale[:, 3:4], w_hi[:, 3], ALU.mult,
                                     ALU.subtract).then_inc(low_split, 1)
            dve.tensor_copy(gate_now[:], gates[:, 0:1]).then_inc(gate_set, 1)
            dve.wait_ge(gate_set, 1)
            dve.wait_ge(scaled, 1)
            project(0, True)
            attention(0, True)
            with dve.Fori(1, B) as i:
                dve.wait_ge(base_ready, TT * i)
                dve.tensor_copy(gate_now[:], gates[:, bass.ds(i, 1)]).then_inc(gate_set, 1)
                dve.wait_ge(out_ready, TT * (i - 1) + 1)
                dve.tensor_copy(gate_before[:], gates_f[:, bass.ds(i - 1, 1)]).then_inc(gate_set, 1)
                dve.wait_ge(gate_set, 2 * i + 1)
                project(i, False)
                feed_1(i - 1)
                attention(i, False)
            dve.wait_ge(out_ready, TT * (B - 1) + 1)
            dve.tensor_copy(gate_before[:], gates_f[:, B - 1:B]).then_inc(gate_set, 1)
            dve.wait_ge(gate_set, 2 * B)
            low(B, ("h2", TT - 1))
            feed_1(B - 1, last_item=True)
            for t in range(TT):
                output_rows(B - 1, t)


_W = "L0_cond_"
_INS = ["x", "condB_gatescore"] + [_W + n for n in ("Wq", "bq", "Wk", "bk", "Wv", "bv", "Wo", "bo", "W1", "b1", "W2",
                                                   "b2", "gamma1", "beta1", "gamma2", "beta2")]


def kernel(**inputs):
    import numpy as np
    import concourse.bacc as bacc
    from concourse.bass_utils import run_bass_kernel_spmd

    nc = bacc.Bacc("TRN2", target_bir_lowering=False, num_devices=1, dynamic_dma_scratch_size=1024)
    arrays, args = {}, []
    for name in _INS:
        a = np.ascontiguousarray(inputs[name])
        arrays["in_" + name] = a
        args.append(nc.dram_tensor("in_" + name, a.shape, mybir.dt.from_np(a.dtype), kind="ExternalInput").ap())
    shape = inputs["x"].shape
    args.append(nc.dram_tensor("out_0", shape, F32, kind="ExternalOutput").ap())
    build(nc, *args)
    r = run_bass_kernel_spmd(nc, [arrays], core_ids=[0])
    return r.results[0]["out_0"]
```

```python
from contextlib import ExitStack

import concourse.bass as bass
from concourse import mybir

ALU = mybir.AluOpType
ACT = mybir.ActivationFunctionType
AX_X = mybir.AxisListType.X
F32 = mybir.dt.float32
F16 = mybir.dt.float16
BF16 = mybir.dt.bfloat16

P = 128
T, C, NH, FF = 512, 512, 16, 2048
DH = C // NH
TT = T // P
DK = C // P
FJ = FF // P
HPT = P // DH
PARTS = 3
EPS = 1e-5
NORM_TO = 1024.0
TINY = 1e-12
LOG_P = 6.931471805599453
MASKED = -1e30

COLS, LATE, CONSTS = 2, 9, 9

GROUPS = [(qt, h0, max(1, TT // (qt + 1) if qt < 2 else 1))
          for qt in range(TT) for h0 in range(0, NH, max(1, TT // (qt + 1) if qt < 2 else 1))]
NG = len(GROUPS)
FIRST = [min(g for g, x in enumerate(GROUPS) if x[0] == qt) for qt in range(TT)]
LAST = [max(g for g, x in enumerate(GROUPS) if x[0] == qt) for qt in range(TT)]
HALF = NH // 2
HALF_FIRST = {(qt, half): min(g for g, x in enumerate(GROUPS) if x[0] == qt and x[1] // HALF == half)
              for qt in range(TT) for half in range(2)}
HALF_LAST = {(qt, half): max(g for g, x in enumerate(GROUPS) if x[0] == qt and x[1] // HALF == half)
             for qt in range(TT) for half in range(2)}
STEPS = NG + 3
TAIL_CTX, TAIL_W, TAIL_ROWS, TAIL_H2 = 1, 3, 4, 7

F_MMS, W_MMS = 3 * FJ, 3 * DK
QUOTA = [16, 3, 3, 3, 3, 3, 3, 3, 4, 4, 3] + [6] * 10 + [5, 5] + [4] * 10 + [5, 5] + [4] * 3 + [5] * 6 + [6] * 3
assert sum(QUOTA) == TT * F_MMS + (TT - 1) * W_MMS and len(QUOTA) == STEPS
CTX_EVAC = {6: (0, 0), 8: (0, 1), 14: (1, 0), 16: (1, 1), 25: (2, 0), 32: (2, 1), 45: (3, 0), STEPS: (3, 1)}
assert all(s >= min(HALF_LAST[part] + 5, STEPS) for s, part in CTX_EVAC.items())
W_AT = {LAST[0] + 8: 0, LAST[1] + 10: 1, LAST[2] + 8: 2}
FILLERS = []
_f = [("F", t, n) for t in range(TT) for n in range(F_MMS)]
_w = []
for _s in range(STEPS):
    if _s in W_AT:
        _w += [("W", W_AT[_s], n) for n in range(W_MMS)]
    _n = min(len(_w), QUOTA[_s])
    FILLERS.append(_w[:_n] + _f[:QUOTA[_s] - _n])
    _w, _f = _w[_n:], _f[QUOTA[_s] - _n:]
assert not _w and not _f


def step_of(kind, t):
    return max(s for s in range(STEPS) if any(x[:2] == (kind, t) for x in FILLERS[s]))


F_EVAC = {step_of("F", t) + 1: t for t in range(TT)}
W_EVAC = {step_of("W", t) + 1: t for t in range(TT - 1)}
W_DONE = [sum(e < s for e in W_EVAC) for s in range(STEPS)]
_W_STEPS = [s for s in range(STEPS) if any(x[0] == "W" for x in FILLERS[s])]
NORMS = {("z", 0): (0, 1, 2), ("z", 1): (2, 3, 4), ("h2", 0): (15, 17, 19), ("z", 2): (22, 23, 25),
         ("h2", 1): (27, 28, 29), ("z", 3): (36, 37, 39), ("h2", 2): (41, 42, 43)}
ROW_ORDER = list(NORMS)
STATS_AT = {at[0]: tile for tile, at in NORMS.items()}
NORM_AT = {at[1]: tile for tile, at in NORMS.items()}
BASE_AT = {at[2]: t for (kind, t), at in NORMS.items() if kind == "h2"}
assert all(NORMS["h2", t][0] >= e + 2 for e, t in W_EVAC.items()) and sorted(STATS_AT) == list(STATS_AT)
SIDE = [[] for _ in range(STEPS)]
for _t in range(TT - 1):
    SIDE[LAST[_t] + 6].append(("ctx", _t))
for _tile, _at in NORMS.items():
    SIDE[_at[2]].append(_tile)
assert max(map(len, SIDE)) == 1 and not any(SIDE[s] for s in _W_STEPS)
assert not any(SIDE[s] and SIDE[s + 1] for s in range(STEPS - 1))
CTX_TURN = {t: s for s in range(STEPS) for kind, t in SIDE[s] if kind == "ctx"}
W_START = {t: s for s, t in W_AT.items()}
assert all(f < w for f, w in zip(F_EVAC, W_EVAC))
QUARTERS = [2, 3, 0, 1]
BETA_AT = {4 + n: range(2 * n, 2 * n + 2) for n in range(FJ // 2)}
SQUARE_1 = {8: 0, 11: 1}
STAT_1 = 12
SPLIT_1 = {STAT_1 + 2 + n: k for n, k in enumerate(QUARTERS)}
SQUARE_2 = {21 + n: k for n, k in enumerate(QUARTERS)}
STAT_2 = 25
SPLIT_2 = {STAT_2 + 2 + n: k for n, k in enumerate(QUARTERS)}
_ORDER = [("ctx", TT - 1), ("h2", TT - 1)] + [job for jobs in SIDE for job in jobs]
assert _ORDER[-1] == ("h2", TT - 2)


def side(i, job):
    return len(_ORDER) * i + (TT - 2) + _ORDER.index(job)


def build(nc, x, gate, wq, bq, wk, bk, wv, bv, wo, bo, w1, b1, w2, b2, gamma1, beta1, gamma2, beta2, out):
    B = x.shape[0]
    x_rows = x.rearrange("b (t p) c -> b t p c", p=P)
    out_rows = out.rearrange("b (t p) c -> b t p c", p=P)

    def column(v):
        return v.rearrange("(c p) -> p c", p=P)

    def row(v):
        return v.rearrange("(a n) -> a n", a=1).to_broadcast([P, v.shape[0]])

    with ExitStack() as ctx:
        def sb(name, shape, dt=F32):
            return ctx.enter_context(nc.sbuf_tensor(name, shape, dt))

        def bank(name):
            return ctx.enter_context(nc.psum_tensor(name, [P, 512], F32))

        def sem(name):
            return ctx.enter_context(nc.semaphore(name))

        w_hi = sb("w_hi", [P, 4, DK, C], F16)
        w_lo = sb("w_lo", [P, 4, DK, C], F16)
        w1_hi, w1_lo = sb("w1_hi", [P, DK, FF], F16), sb("w1_lo", [P, DK, FF], F16)
        w2_hi, w2_lo = sb("w2_hi", [P, FJ, C], F16), sb("w2_lo", [P, FJ, C], F16)
        g_all = sb("g_all", [P, 2, FJ, T], F16)
        g_hi, g_lo = g_all[:, 0], g_all[:, 1]
        qk_parts = g_all[:].rearrange("p a j t -> p (a j) t")[:, 0:4 * DK, :].rearrange(
            "p (m s d) t -> p m s d t", m=2, s=2)
        w_stage = g_all[:].rearrange("p a j t -> p (a j t)").bitcast(F32)
        w1_stage = w_stage.rearrange("p (k n) -> p k n", k=DK)
        w2_stage = w_stage.rearrange("p (j c) -> p j c", j=FJ)
        stacks = sb("stacks", [P, 2, HPT, DK, T], F16)
        qkvo_stage = stacks[:].rearrange("p m j d t -> p (m j d t)").bitcast(F32).rearrange(
            "p (m k c) -> p m k c", m=4, k=DK)
        z_hi, z_lo = sb("z_hi", [P, DK, T], F16), sb("z_lo", [P, DK, T], F16)
        h2_hi, h2_lo = sb("h2_hi", [P, DK, T], F16), sb("h2_lo", [P, DK, T], F16)
        v_all = sb("v_all", [P, TT, NH, 2, DH], F16)
        base = sb("base", [P, TT, C])
        probs = sb("probs", [P, 2, 512])
        pt_hi, pt_lo = sb("pt_hi", [P, 3, 512], F16), sb("pt_lo", [P, 3, 512], F16)
        ctx_rows = sb("ctx_rows", [P, C])
        ctx_hi, ctx_lo = sb("ctx_hi", [P, DK, P], F16), sb("ctx_lo", [P, DK, P], F16)
        att = sb("att", [P, C])
        xn = sb("xn", [P, 2, C])
        x1 = sb("x1", [P, C])
        out_sb = sb("out_sb", [P, C])
        bo_row, b2_row = sb("bo_row", [P, C]), sb("b2_row", [P, C])
        mask = sb("mask", [P, P], BF16)
        ident_b = sb("ident_b", [P, P], BF16)
        ident = sb("ident", [P, P])
        ones = out_sb[:, 0:P]
        bv_wide = att[:].rearrange("p (k n) -> p k n", k=DK)
        sums, rsums = sb("sums", [P, 2, NH]), sb("rsums", [P, NH])
        rmax, umax, nmax = sb("rmax", [P, 2, TT]), sb("umax", [P, 2, TT]), sb("nmax", [P, 2, TT])
        st6, mv = sb("st6", [P, 2, 6]), sb("mv", [P, 2, 2])
        veps, rstd = sb("veps", [P, 2]), sb("rstd", [P, 2])
        gates, gates_f = sb("gates", [P, B]), sb("gates_f", [P, B])
        gate_now, gate_before = sb("gate_now", [P, 1]), sb("gate_before", [P, 1])
        gam1, bet1 = sb("gam1", [P, DK]), sb("bet1", [P, DK])
        gam2, bet2 = sb("gam2", [P, DK]), sb("bet2", [P, DK])
        b_qkv, b_1 = sb("b_qkv", [P, 3, DK]), sb("b_1", [P, FJ])
        bs_qk = sb("bs_qk", [P, 2, DK])
        sq_w, sq_f = sb("sq_w", [P, 4, DK]), sb("sq_f", [P, 2, DK])
        sq_b, red = sb("sq_b", [P, FJ]), sb("red", [P, 2, TT])
        stat, pw, scale = sb("stat", [P, 6]), sb("pw", [P, 6]), sb("scale", [P, 6])
        c_half, c_eps = sb("c_half", [P, 6]), sb("c_eps", [P, 1])
        pad = sb("pad", [P, 1])
        gs = sb("gs", [P, 4, DK])
        exp_scale, exp_wide, log_p = sb("exp_scale", [P, 1]), sb("exp_wide", [P, TT]), sb("log_p", [P, TT])
        co, cf, inv_s1, prod = sb("co", [P, 1]), sb("cf", [P, 1]), sb("inv_s1", [P, 1]), sb("prod", [P, 3])

        score_ps = [bank("score0"), bank("score1")]
        trans_ps = [bank("trans0"), bank("trans1")]
        value_ps = [bank("value0"), bank("value1")]
        dense_ps = [bank("dense0"), bank("dense1")]
        side_ps, ff_ps = dense_ps

        cols_in, x_first = sem("cols_in"), [sem("x_first0"), sem("x_first1")]
        w_in = [sem(f"w_in{m}") for m in range(4)]
        w1_in = [sem("w1_in0"), sem("w1_in1")]
        w2_in = [sem("w2_in0"), sem("w2_in1")]
        late_in = sem("late_in")
        consts_made = sem("consts_made")
        squared = sem("squared")
        biased = sem("biased")
        half_read = sem("half_read")
        stat_part = sem("stat_part")
        summed = sem("summed")
        stat_ready, powered = sem("stat_ready"), sem("powered")
        scaled = sem("scaled")
        chain = sem("chain")
        high_split, low_split = sem("high_split"), sem("low_split")
        bv_ready, bo_filled = sem("bv_ready"), sem("bo_filled")
        x_in = [sem("x_in0"), sem("x_in1")]
        res_in = [sem("res_in0"), sem("res_in1")]
        row_aux, row_stats = sem("row_aux"), sem("row_stats")
        row_veps, row_rstd = sem("row_veps"), sem("row_rstd")
        z_ready, h2_ready = sem("z_ready"), sem("h2_ready")
        side_filled, side_high, side_low = sem("side_filled"), sem("side_high"), sem("side_low")
        p_filled, p_high, p_low = sem("p_filled"), sem("p_high"), sem("p_low")
        qkv_filled, qkv_high, qkv_low = sem("qkv_filled"), sem("qkv_high"), sem("qkv_low")
        stacked = sem("stacked")
        scored, maxed, shifted, neg_ready = sem("scored"), sem("maxed"), sem("shifted"), sem("neg_ready")
        exp_done, valued = sem("exp_done"), sem("valued")
        ctx_copied, ctx_aux, ctx_ready = sem("ctx_copied"), sem("ctx_aux"), sem("ctx_ready")
        wo_filled, att_ready = sem("wo_filled"), sem("att_ready")
        x1_ready, attb_ready, base_ready = sem("x1_ready"), sem("attb_ready"), sem("base_ready")
        gate_set = sem("gate_set")
        f1_filled, gelu_done, g_high, g_low = sem("f1_filled"), sem("gelu_done"), sem("g_high"), sem("g_low")
        f2_filled, out_ready, stored = sem("f2_filled"), sem("out_ready"), sem("stored")

        def hidden_bank(j):
            return trans_ps[1] if j == FJ - 1 else dense_ps[j % 2]

        block = ctx.enter_context(nc.Block())
        STACK_DMAS = 2 * PARTS * HPT
        QKV = 3 * DK
        SPLITS = 3 * DK + 1

        @block.sync
        def _(sp):
            def stack_parts(i, first=False):
                for m, kinds in enumerate(((0, 0, 1), (0, 1, 0))):
                    if first:
                        sp.wait_ge(low_split, (m + 1) * 2 * DK if m == 0 else SPLITS)
                    if first and m == 1:
                        sp.wait_ge(bo_filled, 1)
                    sp.wait_ge(qkv_low, QKV * i + DK * (m + 1))
                    for part, kind in enumerate(kinds):
                        for j in range(HPT):
                            sp.dma_start(stacks[DH * part:DH * (part + 1), m, j],
                                         qk_parts[DH * j:DH * (j + 1), m, kind]).then_inc(stacked, 16)

            def load_x(i, nxt, t):
                before = side(i, ("z", t - 2)) if t >= 2 else side(i - 1, ("z", t + 2))
                sp.wait_ge(side_filled, before + 1)
                sp.dma_start(xn[:, t % 2], x_rows[nxt, t]).then_inc(x_in[t % 2], 16)

            def store_out(f, t):
                sp.wait_ge(out_ready, TT * f + t + 2)
                sp.dma_start(out_rows[f, t], out_sb[:]).then_inc(stored, 16)

            def iteration(i, nxt):
                stack_parts(i)
                load_x(i, nxt, 0)
                load_x(i, nxt, 1)
                for t in range(TT):
                    store_out(i - 1, t)
                    sp.dma_start(base[:, t], x_rows[i, t]).then_inc(res_in[t % 2], 16)
                    if t < 2:
                        load_x(i, nxt, t + 2)

            for tile, v in ((bet1, beta1), (gam1, gamma1)):
                sp.dma_start(tile[:], column(v), allow_slow_non_contiguous=True).then_inc(cols_in, 16)
            for m, w in enumerate((wq, wk, wv, wo)):
                sp.dma_start(qkvo_stage[:, m], w.rearrange("(k p) c -> p k c", p=P)).then_inc(w_in[m], 16)
            w1_rows, w2_rows = w1.rearrange("(k p) n -> p k n", p=P), w2.rearrange("(j p) c -> p j c", p=P)
            sp.wait_ge(late_in, 16 * LATE)
            sp.dma_start(w1_stage[:, DK // 2:], w1_rows[:, DK // 2:]).then_inc(w1_in[1], 16)
            stack_parts(0, True)
            for t in range(2):
                sp.wait_ge(side_filled, t + 3)
                sp.dma_start(xn[:, t], x_rows[1, t]).then_inc(x_in[t], 16)
            sp.wait_ge(stacked, 16 * STACK_DMAS)
            sp.dma_start(w1_stage[:, 0:DK // 2], w1_rows[:, 0:DK // 2]).then_inc(w1_in[0], 16)
            load_x(0, 1, 2)
            load_x(0, 1, 3)
            sp.wait_ge(biased, 3)
            for half in (1, 0):
                sp.wait_ge(low_split, SPLITS + DK // 2 * (2 - half))
                rows = slice(FJ // 2 * half, FJ // 2 * (half + 1))
                sp.dma_start(w2_stage[:, rows], w2_rows[:, rows]).then_inc(w2_in[half], 16)
            with sp.Fori(1, B - 1) as i:
                iteration(i, i + 1)
            iteration(B - 1, B - 1)
            for t in range(TT):
                store_out(B - 1, t)
            sp.wait_ge(stored, 16 * (TT * B + 1))

        @block.gpsimd
        def _(pool):
            pool.memset(c_half[:], -0.5).then_inc(consts_made, 1)
            pool.memset(c_eps[:], EPS).then_inc(consts_made, 1)
            pool.memset(ones, 1.0).then_inc(consts_made, 1)
            pool.memset(ident[:], 0.0).then_inc(consts_made, 1)
            pool.memset(mask[:], 0.0).then_inc(consts_made, 1)
            pool.memset(ident_b[:], 0.0).then_inc(consts_made, 1)
            pool.wait_ge(consts_made, 6)
            pool.affine_select(out=ident_b[:], in_=ident_b[:], compare_op=ALU.not_equal, fill=1.0, base=0,
                               pattern=[[-1, P]], channel_multiplier=1).then_inc(consts_made, 1)
            pool.affine_select(out=ident[:], in_=ident[:], compare_op=ALU.not_equal, fill=1.0, base=0,
                               pattern=[[-1, P]], channel_multiplier=1).then_inc(consts_made, 1)
            pool.affine_select(out=mask[:], in_=mask[:], compare_op=ALU.is_ge, fill=MASKED, base=0,
                               pattern=[[-1, P]], channel_multiplier=1).then_inc(consts_made, 1)

            def inverse_std(n, which):
                pool.wait_ge(row_stats, n)
                pool.tensor_tensor(veps[:, which:which + 1], mv[:, which, 1:2], c_eps[:],
                                   ALU.add).then_inc(row_veps, 1)
                pool.wait_ge(row_veps, n)
                pool.tensor_tensor(rstd[:, which:which + 1], veps[:, which:which + 1], c_half[:, 0:1],
                                   ALU.pow).then_inc(row_rstd, 1)

            def residual_bias(i, t):
                pool.wait_ge(x1_ready, TT * i + t + 1)
                pool.tensor_tensor(att[:], att[:], b2_row[:], ALU.add).then_inc(attb_ready, 1)

            def residual(i, t, first):
                pool.wait_ge(att_ready, TT * i + t + 1)
                if not first:
                    pool.wait_ge(res_in[t % 2], 16 * (TT // 2 * (i - 1) + t // 2 + 1))
                pool.tensor_tensor(x1[:], base[:, t], att[:], ALU.add).then_inc(x1_ready, 1)

            def negate(i, g):
                heads = GROUPS[g][2]
                pool.wait_ge(maxed, NG * i + g + 1)
                pool.tensor_tensor(umax[:, g % 2, 0:heads], log_p[:, 0:heads], rmax[:, g % 2, 0:heads],
                                   ALU.subtract).then_inc(shifted, 1)
                pool.wait_ge(shifted, NG * i + g + 1)
                pool.tensor_tensor(nmax[:, g % 2, 0:heads], umax[:, g % 2, 0:heads], exp_wide[:, 0:heads],
                                   ALU.mult).then_inc(neg_ready, 1)

            def tail(i):
                residual(i - 1, TT - 1, False)
                residual_bias(i - 1, TT - 1)
                inverse_std(TT + 2 * TT * i, 1)

            def attention(i, first):
                n = TT + 2 * TT * i
                if first:
                    pool.wait_ge(scaled, 2)
                negate(i, 0)
                for s in range(STEPS):
                    if s + 1 < NG:
                        negate(i, s + 1)
                    if first and s in (STAT_1 + 1, STAT_2 + 1):
                        k = 4 if s == STAT_1 + 1 else 5
                        pool.wait_ge(stat_ready, k - 2)
                        pool.tensor_tensor(pw[:, k:k + 1], stat[:, k:k + 1], c_half[:, 0:1],
                                           ALU.pow).then_inc(powered, 1)
                    if s - 1 in W_EVAC:
                        residual(i, W_EVAC[s - 1], first)
                    if s - 2 in W_EVAC:
                        residual_bias(i, W_EVAC[s - 2])
                    if s in STATS_AT:
                        inverse_std(n + ROW_ORDER.index(STATS_AT[s]) + 1, int(STATS_AT[s][0] == "h2"))

            for t in range(TT):
                inverse_std(t + 1, t % 2)
            pool.wait_ge(stat_ready, 1)
            pool.tensor_tensor(pw[:, 0:4], stat[:, 0:4], c_half[:, 0:4], ALU.pow).then_inc(powered, 1)
            attention(0, True)
            residual(0, TT - 1, True)
            residual_bias(0, TT - 1)
            inverse_std(3 * TT, 1)
            with pool.Fori(1, B) as i:
                attention(i, False)
                tail(i + 1)

        @block.scalar
        def _(act):
            def high(i, job):
                act.wait_ge(side_filled, side(i, job) + 1)
                high_of(*job, trans_ps[0] if job[1] == TT - 1 and job[0] != "z" else side_ps)

            def probs_high(i, g):
                width = GROUPS[g][2] * (GROUPS[g][0] + 1) * P
                act.wait_ge(p_filled, NG * i + g + 1)
                act.activation(pt_hi[:, g % 3, 0:width], trans_ps[g % 2][:, 0:width], ACT.Copy).then_inc(p_high, 1)

            def high_of(kind, n, ps):
                dst = {"ctx": ctx_hi, "z": z_hi, "h2": h2_hi}[kind]
                dst = dst[:] if kind == "ctx" else dst[:, :, n * P:(n + 1) * P]
                act.activation(dst, ps[:].rearrange("p (k t) -> p k t", k=DK), ACT.Copy).then_inc(side_high, 1)

            def project(i, first):
                for j in range(QKV):
                    m, n = j // DK, j % DK
                    act.wait_ge(qkv_filled, QKV * i + j + 1)
                    if m < 2:
                        act.activation(qk_parts[:, m, 0, n], dense_ps[j % 2][:], ACT.Identity,
                                       bias=bs_qk[:, m, n:n + 1]).then_inc(qkv_high, 1)
                    else:
                        act.activation(v_all[:, n, :, 0], dense_ps[j % 2][:].rearrange("p (h d) -> p h d", h=NH),
                                       ACT.Copy).then_inc(qkv_high, 1)
                    if j == TAIL_CTX and not first:
                        high(i, ("ctx", TT - 1))
                    if j == TAIL_H2 and not first:
                        high(i, ("h2", TT - 1))
                    if first and j < DK:
                        split_high(2, j)
                    if first and j == DK:
                        split_high(3, 0)
                    if first and j in (DK + 2, DK + 3):
                        act.wait_ge(w1_in[1], 16)
                        square_1(j - DK)

            def feed_1(f):
                for j in range(FJ):
                    act.wait_ge(f1_filled, FJ * f + j + 1)
                    if j >= 2:
                        act.wait_ge(g_low, FJ * f + j - 1)
                    act.activation(probs[:, j % 2], hidden_bank(j)[:], ACT.Gelu, bias=b_1[:, j:j + 1],
                                   scale=inv_s1[:]).then_inc(gelu_done, 1)

            def exps(i, g, first):
                qt, h0, heads = GROUPS[g]
                width = (qt + 1) * P
                act.wait_ge(neg_ready, NG * i + g + 1)
                if g < 2 and not first:
                    act.wait_ge(g_low, FJ * i - 1 + g)
                if g == FIRST[qt] and (qt >= 2 or not first):
                    act.wait_ge(ctx_ready, 2 * (TT * i + qt - 1))
                for a in range(heads):
                    e = act.activation(probs[:, g % 2, a * width:(a + 1) * width],
                                       score_ps[g % 2][:, a * width:(a + 1) * width], ACT.Exp,
                                       bias=nmax[:, g % 2, a:a + 1], scale=exp_scale[:],
                                       accum_out=sums[:, qt % 2, h0 + a:h0 + a + 1])
                e.then_inc(exp_done, 1)

            def square_1(k):
                act.activation(w1_hi[:, k], w1_stage[:, k], ACT.Square, scale=gam2[:, k:k + 1],
                               accum_out=sq_f[:, 0, k:k + 1]).then_inc(squared, 1)

            def square(m):
                act.wait_ge(w_in[m], 16)
                if m == 3:
                    act.activation(w_hi[:, 3], qkvo_stage[:, 3], ACT.Square,
                                   accum_out=sq_w[:, 3, 0:1]).then_inc(squared, 1)
                    return
                for k in range(DK):
                    act.activation(w_hi[:, m, k], qkvo_stage[:, m, k], ACT.Square, scale=gam1[:, k:k + 1],
                                   accum_out=sq_w[:, m, k:k + 1]).then_inc(squared, 1)

            def split_high(m, k):
                if m == 3:
                    act.activation(w_hi[:, 3], qkvo_stage[:, 3], ACT.Copy,
                                   scale=scale[:, 3:4]).then_inc(high_split, 1)
                    return
                act.activation(w_hi[:, m, k], qkvo_stage[:, m, k], ACT.Copy,
                               scale=gs[:, m, k:k + 1]).then_inc(high_split, 1)

            def item_0_rows(tiles):
                for t in tiles:
                    act.wait_ge(side_filled, t + 1)
                    high_of("z", t, trans_ps[t % 2])

            def context_copy(i, qt, half):
                n = 2 * (TT * i + qt) + half + 1
                act.wait_ge(valued, n)
                act.activation(ctx_rows[:].rearrange("p (h d) -> p h d", h=NH)[:, HALF * half:HALF * (half + 1)],
                               value_ps[half][:].rearrange("p (h m d) -> p h m d", h=HALF, m=2)[:, :, 0],
                               ACT.Copy).then_inc(ctx_copied, 1)

            def attention(i, first):
                for s in range(STEPS):
                    if s < NG:
                        exps(i, s, first)
                    if 1 <= s <= NG:
                        probs_high(i, s - 1)
                    for job in SIDE[s]:
                        high(i, job)
                    if s + 1 in CTX_EVAC and s + 1 < STEPS:
                        context_copy(i, *CTX_EVAC[s + 1])
                    if first:
                        if s in SQUARE_1:
                            act.wait_ge(w1_in[0], 16)
                            square_1(SQUARE_1[s])
                        if s in SPLIT_1:
                            k = SPLIT_1[s]
                            act.wait_ge(scaled, 3)
                            act.activation(w1_hi[:, k], w1_stage[:, k], ACT.Copy,
                                           scale=gs[:, 3, k:k + 1]).then_inc(high_split, 1)
                        if s in SQUARE_2:
                            k = SQUARE_2[s]
                            act.wait_ge(w2_in[k // 2], 16)
                            act.activation(w2_hi[:, 4 * k:4 * k + 4], w2_stage[:, 4 * k:4 * k + 4], ACT.Square,
                                           accum_out=sq_f[:, 1, k:k + 1]).then_inc(squared, 1)
                        if s in SPLIT_2:
                            k = SPLIT_2[s]
                            act.wait_ge(scaled, 4)
                            act.activation(w2_hi[:, 4 * k:4 * k + 4], w2_stage[:, 4 * k:4 * k + 4], ACT.Copy,
                                           scale=scale[:, 5:6]).then_inc(high_split, 1)
                context_copy(i, TT - 1, 1)

            x_tiles = x_rows[0].rearrange("t p c -> p t c")
            for t in range(0, TT, 2):
                act.dma_start(base[:, t:t + 2], x_tiles[:, t:t + 2]).then_inc(x_first[t // 2], 16)
            for m, v in enumerate((bq, bk, bv)):
                act.dma_start(b_qkv[:, m], column(v), allow_slow_non_contiguous=True).then_inc(late_in, 16)
            for tile, v in ((gam2, gamma2), (bet2, beta2), (b_1, b1)):
                act.dma_start(tile[:], column(v), allow_slow_non_contiguous=True).then_inc(late_in, 16)
            act.dma_start(bo_row[:], row(bo)).then_inc(late_in, 16)
            act.dma_start(b2_row[:], row(b2)).then_inc(late_in, 16)
            act.dma_start(gates[:], row(gate)).then_inc(late_in, 16)
            item_0_rows((0, 1))
            act.wait_ge(cols_in, 16 * COLS)
            square(0)
            item_0_rows((2, 3))
            for m in range(1, 4):
                square(m)
            act.wait_ge(scaled, 1)
            for m in range(2):
                for k in range(DK):
                    split_high(m, k)
            act.wait_ge(scaled, 2)
            act.wait_ge(late_in, 16 * LATE)
            project(0, True)
            attention(0, True)
            with act.Fori(1, B) as i:
                project(i, False)
                feed_1(i - 1)
                attention(i, False)
            high(B, ("ctx", TT - 1))
            high(B, ("h2", TT - 1))
            feed_1(B - 1)

        @block.tensor
        def _(pe):
            def turn(ps, src, filled):
                for b, block_in in enumerate(src):
                    last = pe.transpose(ps[:, b * P:(b + 1) * P], block_in, ident[:])
                last.then_inc(filled, 1)

            def probs_turn(i, g, first):
                pe.wait_ge(exp_done, NG * i + g + 1)
                if g >= 2 or not first:
                    pe.wait_ge(p_low, NG * i + g - 1)
                if g == 1 and not first:
                    pe.wait_ge(gelu_done, FJ * i)
                turn(trans_ps[g % 2], [probs[:, g % 2, b * P:(b + 1) * P]
                                       for b in range(GROUPS[g][2] * (GROUPS[g][0] + 1))], p_filled)

            def side_turn(i, job, ps):
                kind, n = job
                if kind == "ctx":
                    pe.wait_ge(ctx_ready, 2 * (TT * (i - (n == TT - 1)) + n + 1))
                    rows = ctx_rows[:]
                elif kind == "z":
                    pe.wait_ge(z_ready, TT * (i + 1) + n + 1)
                    rows = xn[:, n % 2]
                else:
                    pe.wait_ge(h2_ready, TT * (i - (n == TT - 1)) + n + 1)
                    rows = x1[:]
                turn(ps, [rows[:, k * P:(k + 1) * P] for k in range(DK)], side_filled)

            def tail_step(i, j):
                if j == TAIL_CTX:
                    pe.wait_ge(p_low, NG * i)
                    side_turn(i, ("ctx", TT - 1), trans_ps[0])
                if j == TAIL_W:
                    for n in range(W_MMS):
                        output(i - 1, TT - 1, n, trans_ps[1])
                if j == TAIL_H2:
                    side_turn(i, ("h2", TT - 1), trans_ps[0])

            def project(i, first):
                pe.wait_ge(side_low, TT if first else side(i - 1, ("h2", TT - 2)) + 1)
                for j in range(QKV):
                    m, n = j // DK, j % DK
                    if first and n == 0:
                        pe.wait_ge(low_split, DK * (m + 1))
                    ps = dense_ps[j % 2]
                    if j >= 2:
                        pe.wait_ge(qkv_low, QKV * i + j - 1)
                    elif j == 1 and not first:
                        pe.wait_ge(out_ready, TT * i - TT + 1)
                    for k in range(DK):
                        for ws, zs in ((w_hi, z_hi), (w_hi, z_lo), (w_lo, z_hi)):
                            if m < 2:
                                a, b = ws[:, m, k, n * P:(n + 1) * P], zs[:, k]
                            else:
                                a, b = zs[:, k, n * P:(n + 1) * P], ws[:, m, k]
                            last = pe.matmul(ps[:], a, b, start=(k == 0 and ws is w_hi and zs is z_hi),
                                             stop=(k == DK - 1 and ws is w_lo))
                    last.then_inc(qkv_filled, 1)
                    if not first:
                        tail_step(i, j)
                    if first and j == DK:
                        pe.wait_ge(late_in, 16 * LATE)
                        pe.wait_ge(w1_in[1], 16)
                        beta_2(score_ps[0], range(FJ), QUARTERS[:2]).then_inc(biased, 1)

            def feed_1(f, last_item=False):
                pe.wait_ge(side_low, side(f + 1, ("h2", TT - 1)) + 1)
                for j in range(FJ):
                    ps = hidden_bank(j)
                    if j == FJ - 2 and not last_item:
                        scores(f + 1, 0, False)
                    if j >= 2:
                        pe.wait_ge(gelu_done, FJ * f + j - 1)
                    elif not last_item:
                        pe.wait_ge(qkv_low, QKV * (f + 2) - 1 + j)
                    elif j == 1:
                        pe.wait_ge(out_ready, TT * f + 1)
                    if j == FJ - 1:
                        pe.wait_ge(att_ready, TT * (f + 1))
                    for k in range(DK):
                        for n, (ws, hs) in enumerate(((w1_hi, h2_hi), (w1_hi, h2_lo), (w1_lo, h2_hi))):
                            last = pe.matmul(ps[:], ws[:, k, j * P:(j + 1) * P], hs[:, k],
                                             start=(k == 0 and n == 0), stop=(k == DK - 1 and n == 2))
                    last.then_inc(f1_filled, 1)

            def feed_2(f, t, n):
                if n == 0 and t == 0:
                    pe.wait_ge(g_low, FJ * (f + 1) - 2)
                elif n == F_MMS - 6 and t == 0:
                    pe.wait_ge(g_low, FJ * (f + 1))
                elif n == 0:
                    pe.wait_ge(out_ready, TT * f + t + 1)
                j = n // 3
                gsrc, wsrc = ((g_hi, w2_hi), (g_hi, w2_lo), (g_lo, w2_hi))[n % 3]
                mm = pe.matmul(ff_ps[:], gsrc[:, j, t * P:(t + 1) * P], wsrc[:, j],
                               start=(n == 0), stop=(n == F_MMS - 1))
                if n == F_MMS - 1:
                    mm.then_inc(f2_filled, 1)

            def output(i, t, n, ps):
                if n == 0:
                    pe.wait_ge(side_low, side(i + (t == TT - 1), ("ctx", t)) + 1 + (
                        sum(map(len, SIDE[CTX_TURN[t] + 1:W_START[t]])) if t < TT - 1 else 0))
                k = n // 3
                csrc, wsrc = ((ctx_hi, w_hi), (ctx_hi, w_lo), (ctx_lo, w_hi))[n % 3]
                mm = pe.matmul(ps[:], csrc[:, k], wsrc[:, 3, k], start=(n == 0), stop=(n == W_MMS - 1))
                if n == W_MMS - 1:
                    mm.then_inc(wo_filled, 1)

            def dense(i, first, jobs):
                for kind, t, n in jobs:
                    if kind == "W":
                        output(i, t, n, side_ps)
                    elif not first:
                        feed_2(i - 1, t, n)

            def scores(i, g, first):
                qt, h0, heads = GROUPS[g]
                width = (qt + 1) * P
                if g == 0:
                    pe.wait_ge(stacked, 16 * STACK_DMAS * (i + 1))
                if g >= 2 or not first:
                    pe.wait_ge(exp_done, NG * i + g - 1)
                for a in range(heads):
                    dt, j = divmod(h0 + a, HPT)
                    pe.matmul(score_ps[g % 2][:, a * width:(a + 1) * width],
                              stacks[0:PARTS * DH, 0, j, dt, qt * P:(qt + 1) * P],
                              stacks[0:PARTS * DH, 1, j, dt, 0:width], start=True, stop=False,
                              skip_group_check=True)
                    last = pe.matmul(score_ps[g % 2][:, a * width + qt * P:(a + 1) * width], ident_b[:], mask[:],
                                     start=False, stop=True, skip_group_check=True)
                last.then_inc(scored, 1)

            def values(i, g, first):
                qt, h0, heads = GROUPS[g]
                pe.wait_ge(p_low, NG * i + g + 1)
                half = h0 // HALF
                if g == HALF_FIRST[qt, half] and (qt >= 1 or not first):
                    pe.wait_ge(ctx_ready, 2 * (TT * i + qt - 1) + half + 1)
                ps = value_ps[half][:].rearrange("p (h m d) -> p h m d", h=HALF, m=2)
                for a in range(heads):
                    h = h0 + a
                    for kt in range(qt + 1):
                        b = slice((a * (qt + 1) + kt) * P, (a * (qt + 1) + kt + 1) * P)
                        pe.matmul(ps[:, h % HALF], pt_hi[:, g % 3, b], v_all[:, kt, h],
                                  start=(g == HALF_FIRST[qt, half] and a == 0 and kt == 0), stop=False,
                                  skip_group_check=True)
                        last = pe.matmul(ps[:, h % HALF, 1], pt_lo[:, g % 3, b], v_all[:, kt, h, 0], start=False,
                                         stop=(g == HALF_LAST[qt, half] and a == heads - 1 and kt == qt),
                                         skip_group_check=True)
                if g == HALF_LAST[qt, half]:
                    last.then_inc(valued, 1)

            def ff_setup(s):
                if s in BETA_AT:
                    if s == min(BETA_AT):
                        pe.wait_ge(w1_in[0], 16)
                        pe.wait_ge(qkv_low, QKV)
                    last = beta_2(ff_ps, BETA_AT[s], QUARTERS[2:])
                    if s == max(BETA_AT):
                        last.then_inc(biased, 1)
                if s in (STAT_1 + 1, STAT_2 + 1):
                    k = 4 if s == STAT_1 + 1 else 5
                    pe.wait_ge(stat_part, k - 2)
                    pe.matmul(ff_ps[:, k:k + 1], ones, stat[:, k:k + 1], start=True, stop=True,
                              skip_group_check=True).then_inc(summed, 1)

            def attention(i, first):
                if first:
                    pe.wait_ge(half_read, 1)
                    scores(i, 0, first)
                for s in range(STEPS):
                    jobs = FILLERS[s]
                    half = (len(jobs) + 1) // 2
                    if s + 1 < NG:
                        scores(i, s + 1, first)
                    if 1 <= s <= NG:
                        probs_turn(i, s - 1, first)
                    dense(i, first, jobs[:half])
                    for job in SIDE[s]:
                        if job == ("z", 0):
                            pe.wait_ge(qkv_low if first else gelu_done, QKV if first else FJ * i)
                        else:
                            pe.wait_ge(side_low, side(i, job))
                        if W_DONE[s]:
                            pe.wait_ge(att_ready, TT * i + W_DONE[s])
                        side_turn(i, job, side_ps)
                    dense(i, first, jobs[half:])
                    if 3 <= s < NG + 3:
                        values(i, s - 3, first)
                    if first:
                        ff_setup(s)

            pe.wait_ge(consts_made, CONSTS)
            def beta_2(ps, tiles, quarters):
                for j in tiles:
                    for k in quarters:
                        last = pe.matmul(ps[:, j:j + 1], w1_stage[:, k, j * P:(j + 1) * P], bet2[:, k:k + 1],
                                         start=(k == quarters[0]), stop=(k == quarters[-1]))
                return last

            def item_0_rows(tiles):
                for t in tiles:
                    pe.wait_ge(z_ready, t + 1)
                    if t >= 2:
                        pe.wait_ge(side_low, t - 1)
                    turn(trans_ps[t % 2], [xn[:, t % 2, k * P:(k + 1) * P] for k in range(DK)], side_filled)

            item_0_rows((0, 1))
            pe.wait_ge(cols_in, 16 * COLS)
            for m in range(3):
                pe.wait_ge(w_in[m], 16)
                for n in range(DK):
                    for k in range(DK):
                        last = pe.matmul(value_ps[0][:, m * DK + n:m * DK + n + 1],
                                         qkvo_stage[:, m, k, n * P:(n + 1) * P], bet1[:, k:k + 1],
                                         start=(k == 0), stop=(k == DK - 1))
                if m == 0:
                    item_0_rows((2, 3))
            last.then_inc(biased, 1)
            pe.wait_ge(stat_part, 1)
            pe.matmul(value_ps[1][:, 0:4], ones, stat[:, 0:4], start=True, stop=True).then_inc(summed, 1)
            pe.wait_ge(bv_ready, DK)
            pe.wait_ge(w_in[3], 16)
            for k in range(DK):
                last = pe.matmul(value_ps[0][:], bv_wide[:, k], qkvo_stage[:, 3, k], start=(k == 0),
                                 stop=(k == DK - 1))
            last.then_inc(bo_filled, 1)
            project(0, True)
            attention(0, True)
            with pe.Fori(1, B) as i:
                project(i, False)
                feed_1(i - 1)
                attention(i, False)
            for j in range(QKV):
                tail_step(B, j)
            feed_1(B - 1, last_item=True)
            for t in range(TT):
                for n in range(F_MMS):
                    feed_2(B - 1, t, n)

        @block.vector
        def _(dve):
            steps = [0]

            def link(ins):
                steps[0] += 1
                ins.then_inc(chain, 1)
                dve.wait_ge(chain, steps[0])

            def low_of(kind, n, ps):
                hi, lo = {"ctx": (ctx_hi, ctx_lo), "z": (z_hi, z_lo), "h2": (h2_hi, h2_lo)}[kind]
                cols = slice(0, P) if kind == "ctx" else slice(n * P, (n + 1) * P)
                dve.tensor_tensor(lo[:, :, cols], ps[:].rearrange("p (k t) -> p k t", k=DK),
                                  hi[:, :, cols], ALU.subtract).then_inc(side_low, 1)

            def low(i, job):
                dve.wait_ge(side_high, side(i, job) + 1)
                low_of(*job, trans_ps[0] if job[1] == TT - 1 and job[0] != "z" else side_ps)

            def probs_low(i, g):
                width = GROUPS[g][2] * (GROUPS[g][0] + 1) * P
                dve.wait_ge(p_high, NG * i + g + 1)
                dve.tensor_tensor(pt_lo[:, g % 3, 0:width], trans_ps[g % 2][:, 0:width],
                                  pt_hi[:, g % 3, 0:width], ALU.subtract).then_inc(p_low, 1)

            def tail_step(i, j):
                if j == TAIL_CTX:
                    low(i, ("ctx", TT - 1))
                if j == TAIL_W:
                    attention_rows(i - 1, TT - 1, trans_ps[1])
                if j == TAIL_ROWS:
                    dve.wait_ge(x1_ready, TT * i)
                    row_statistics(TT + 2 * TT * i, 1, x1[:])
                if j == TAIL_ROWS + 1:
                    base_rows(i - 1, TT - 1)
                    norm(TT + 2 * TT * i, 1, x1[:], x1[:], h2_ready)
                if j == TAIL_H2:
                    low(i, ("h2", TT - 1))

            def row_statistics(n, which, rows):
                dve.bn_stats(st6[:, which], rows).then_inc(row_aux, 1)
                dve.wait_ge(row_aux, n)
                dve.memset(pad[:], 0.0)
                dve.bn_aggr(mv[:, which], st6[:, which]).then_inc(row_stats, 1)

            def norm(n, which, dst, rows, ready):
                dve.wait_ge(row_rstd, n)
                dve.tensor_scalar(dst, rows, mv[:, which, 0:1], rstd[:, which:which + 1], ALU.subtract,
                                  ALU.mult).then_inc(ready, 1)

            def project(i, first):
                for j in range(QKV):
                    m, n = j // DK, j % DK
                    dve.wait_ge(qkv_high, QKV * i + j + 1)
                    if m < 2:
                        dve.scalar_tensor_tensor(qk_parts[:, m, 1, n], dense_ps[j % 2][:], bs_qk[:, m, n:n + 1],
                                                 qk_parts[:, m, 0, n], ALU.add, ALU.subtract).then_inc(qkv_low, 1)
                    else:
                        dve.tensor_tensor(v_all[:, n, :, 1],
                                          dense_ps[j % 2][:].rearrange("p (h d) -> p h d", h=NH), v_all[:, n, :, 0],
                                          ALU.subtract).then_inc(qkv_low, 1)
                    if not first:
                        tail_step(i, j)
                    if first and j < DK:
                        split_low(2, j)
                    if first and j == DK:
                        split_low(3, 0)
                    if first and j == DK + 2:
                        dve.wait_ge(bo_filled, 1)
                        link(dve.tensor_tensor(bo_row[:], bo_row[:], value_ps[0][:], ALU.add))
                        dve.wait_ge(biased, 2)
                        dve.tensor_tensor(b_1[:], b_1[:], score_ps[0][:, 0:FJ], ALU.add).then_inc(half_read, 1)

            def split_low(m, k):
                dve.wait_ge(high_split, m * DK + k + 1)
                if m == 3:
                    dve.scalar_tensor_tensor(w_lo[:, 3], qkvo_stage[:, 3], scale[:, 3:4], w_hi[:, 3], ALU.mult,
                                             ALU.subtract).then_inc(low_split, 1)
                    return
                dve.scalar_tensor_tensor(w_lo[:, m, k], qkvo_stage[:, m, k], gs[:, m, k:k + 1], w_hi[:, m, k],
                                         ALU.mult, ALU.subtract).then_inc(low_split, 1)

            def feed_1(f, last_item=False):
                for j in range(FJ):
                    if j == FJ - 2 and not last_item:
                        maxima(f + 1, 0)
                    dve.wait_ge(gelu_done, FJ * f + j + 1)
                    if j == 0 and not last_item:
                        dve.wait_ge(stacked, 16 * STACK_DMAS * (f + 2))
                    dve.tensor_scalar(g_hi[:, j], probs[:, j % 2], scale[:, 4:5], None,
                                      ALU.mult).then_inc(g_high, 1)
                    dve.wait_ge(g_high, FJ * f + j + 1)
                    dve.scalar_tensor_tensor(g_lo[:, j], probs[:, j % 2], scale[:, 4:5], g_hi[:, j],
                                             ALU.mult, ALU.subtract).then_inc(g_low, 1)

            def maxima(i, g):
                qt, h0, heads = GROUPS[g]
                width = (qt + 1) * P
                ps = score_ps[g % 2][:, 0:heads * width].rearrange("p (a k) -> p a k", a=heads)
                dve.wait_ge(scored, NG * i + g + 1)
                dve.tensor_reduce(rmax[:, g % 2, 0:heads], ps, AX_X, ALU.max).then_inc(maxed, 1)

            def context(i, qt, half):
                n = 2 * (TT * i + qt) + half + 1
                heads = slice(HALF * half, HALF * (half + 1))
                rows = ctx_rows[:].rearrange("p (h d) -> p h d", h=NH)[:, heads]
                ps = value_ps[half][:].rearrange("p (h m d) -> p h m d", h=HALF, m=2)
                dve.wait_ge(exp_done, NG * i + HALF_LAST[qt, half] + 1)
                dve.reciprocal(rsums[:, heads], sums[:, qt % 2, heads]).then_inc(ctx_aux, 1)
                dve.wait_ge(ctx_copied, n)
                dve.tensor_tensor(rows, rows, ps[:, :, 1], ALU.add).then_inc(ctx_aux, 1)
                dve.wait_ge(ctx_aux, 2 * n)
                dve.tensor_tensor(rows, rows, rsums[:, heads].unsqueeze(2).to_broadcast([P, HALF, DH]),
                                  ALU.mult).then_inc(ctx_ready, 1)

            def attention_rows(i, t, ps):
                dve.wait_ge(wo_filled, TT * i + t + 1)
                dve.scalar_tensor_tensor(att[:], ps[:], co[:], bo_row[:], ALU.mult,
                                         ALU.add).then_inc(att_ready, 1)

            def base_rows(i, t):
                dve.wait_ge(attb_ready, TT * i + t + 1)
                dve.scalar_tensor_tensor(base[:, t], att[:], gate_now[:], base[:, t], ALU.mult,
                                         ALU.add).then_inc(base_ready, 1)

            def output_rows(f, t):
                dve.wait_ge(f2_filled, TT * f + t + 1)
                dve.wait_ge(base_ready, TT * (f + 1))
                dve.wait_ge(stored, 16 * (TT * f + t + 1))
                dve.scalar_tensor_tensor(out_sb[:], ff_ps[:], gate_before[:], base[:, t], ALU.mult,
                                         ALU.add).then_inc(out_ready, 1)

            def ff_setup(s):
                if s == STAT_1:
                    dve.wait_ge(biased, 3)
                    dve.wait_ge(half_read, 1)
                    link(dve.tensor_tensor(b_1[:], b_1[:], ff_ps[:, 0:FJ], ALU.add))
                    link(dve.tensor_tensor(sq_b[:], b_1[:], b_1[:], ALU.mult))
                    link(dve.tensor_reduce(red[:, 0, 0:1], sq_b[:], AX_X, ALU.add))
                    dve.wait_ge(squared, SPLITS + DK)
                    link(dve.tensor_reduce(red[:, 1, 0:1], sq_f[:, 0], AX_X, ALU.add))
                    dve.scalar_tensor_tensor(stat[:, 4:5], red[:, 0, 0:1], 1.0 / C, red[:, 1, 0:1], ALU.mult,
                                             ALU.add).then_inc(stat_part, 1)
                if s == STAT_2:
                    dve.wait_ge(squared, SPLITS + 2 * DK)
                    dve.tensor_reduce(stat[:, 5:6], sq_f[:, 1], AX_X, ALU.add).then_inc(stat_part, 1)
                if s in (STAT_1 + 1, STAT_2 + 1):
                    k = 4 if s == STAT_1 + 1 else 5
                    dve.wait_ge(summed, k - 2)
                    dve.tensor_scalar(stat[:, k:k + 1], ff_ps[:, k:k + 1], TINY, None,
                                      ALU.add).then_inc(stat_ready, 1)
                    dve.wait_ge(powered, k - 2)
                    link(dve.tensor_scalar(scale[:, k:k + 1], pw[:, k:k + 1], NORM_TO, None, ALU.mult))
                    if k == 4:
                        link(dve.reciprocal(inv_s1[:], scale[:, 4:5]))
                        dve.tensor_scalar(gs[:, 3], gam2[:], scale[:, 4:5], None, ALU.mult).then_inc(scaled, 1)
                    else:
                        dve.memset(pad[:], 0.0).then_inc(stored, 16)
                        link(dve.tensor_tensor(prod[:, 2:3], scale[:, 4:5], scale[:, 5:6], ALU.mult))
                        dve.reciprocal(cf[:], prod[:, 2:3]).then_inc(out_ready, 1)
                        dve.wait_ge(out_ready, 1)
                        dve.tensor_scalar(gates_f[:], gates[:], cf[:], None, ALU.mult).then_inc(scaled, 1)

                if s in SPLIT_1:
                    k = SPLIT_1[s]
                    dve.wait_ge(high_split, SPLITS + QUARTERS.index(k) + 1)
                    dve.scalar_tensor_tensor(w1_lo[:, k], w1_stage[:, k], gs[:, 3, k:k + 1], w1_hi[:, k],
                                             ALU.mult, ALU.subtract).then_inc(low_split, 1)
                if s in SPLIT_2:
                    k = SPLIT_2[s]
                    dve.wait_ge(high_split, SPLITS + DK + QUARTERS.index(k) + 1)
                    rows = slice(4 * k, 4 * k + 4)
                    dve.scalar_tensor_tensor(w2_lo[:, rows], w2_stage[:, rows], scale[:, 5:6], w2_hi[:, rows],
                                             ALU.mult, ALU.subtract).then_inc(low_split, 1)

            def attention(i, first):
                n = TT + 2 * TT * i
                if first:
                    maxima(i, 0)
                for s in range(STEPS):
                    if s in F_EVAC and not first:
                        output_rows(i - 1, F_EVAC[s])
                    if s + 1 < NG:
                        maxima(i, s + 1)
                    if 2 <= s <= NG + 1:
                        probs_low(i, s - 2)
                    if s > 0:
                        for job in SIDE[s - 1]:
                            low(i, job)
                    if s in CTX_EVAC:
                        context(i, *CTX_EVAC[s])
                    if s in W_EVAC:
                        attention_rows(i, W_EVAC[s], side_ps)
                    if s in STATS_AT:
                        kind, t = STATS_AT[s]
                        if kind == "h2":
                            dve.wait_ge(x1_ready, TT * i + t + 1)
                            row_statistics(n + ROW_ORDER.index((kind, t)) + 1, 1, x1[:])
                        else:
                            dve.wait_ge(x_in[t % 2], 16 * (TT // 2 * i + t // 2 + 1))
                            row_statistics(n + ROW_ORDER.index((kind, t)) + 1, 0, xn[:, t % 2])
                    if s in NORM_AT:
                        kind, t = NORM_AT[s]
                        row = n + ROW_ORDER.index((kind, t)) + 1
                        if kind == "h2":
                            norm(row, 1, x1[:], x1[:], h2_ready)
                        else:
                            norm(row, 0, xn[:, t % 2], xn[:, t % 2], z_ready)
                    if s in BASE_AT:
                        base_rows(i, BASE_AT[s])
                    if first:
                        ff_setup(s)
                context(i, TT - 1, 1)
                if not first:
                    output_rows(i - 1, TT - 1)

            for t in range(0, TT, 2):
                dve.wait_ge(x_first[t // 2], 16)
                row_statistics(t + 1, 0, base[:, t])
                row_statistics(t + 2, 1, base[:, t + 1])
                for u in (t, t + 1):
                    if t >= 2:
                        dve.wait_ge(side_filled, u - 1)
                    norm(u + 1, u % 2, xn[:, u % 2], base[:, u], z_ready)
                for u in (t, t + 1):
                    dve.wait_ge(side_high, u + 1)
                    low_of("z", u, trans_ps[u % 2])
            dve.wait_ge(consts_made, CONSTS)
            dve.wait_ge(cols_in, 16 * COLS)
            dve.wait_ge(late_in, 16 * LATE)
            dve.wait_ge(biased, 1)
            link(dve.tensor_tensor(b_qkv[:].rearrange("p m k -> p (m k)"), b_qkv[:].rearrange("p m k -> p (m k)"),
                                   value_ps[0][:, 0:3 * DK], ALU.add))
            link(dve.tensor_tensor(sq_b[:, 0:3 * DK], b_qkv[:].rearrange("p m k -> p (m k)"),
                                   b_qkv[:].rearrange("p m k -> p (m k)"), ALU.mult))
            link(dve.tensor_reduce(red[:, 0, 0:3], sq_b[:, 0:3 * DK].rearrange("p (m k) -> p m k", m=3), AX_X, ALU.add))
            dve.wait_ge(squared, SPLITS)
            dve.tensor_copy(stat[:, 3:4], sq_w[:, 3, 0:1])
            link(dve.tensor_reduce(red[:, 1, 0:3], sq_w[:, 0:3], AX_X, ALU.add))
            dve.scalar_tensor_tensor(stat[:, 0:3], red[:, 0, 0:3], 1.0 / C, red[:, 1, 0:3], ALU.mult,
                                     ALU.add).then_inc(stat_part, 1)
            dve.wait_ge(summed, 1)
            dve.tensor_scalar(stat[:, 0:4], value_ps[1][:, 0:4], TINY, None, ALU.add).then_inc(stat_ready, 1)
            for k in range(DK):
                dve.tensor_copy(bv_wide[:, k], b_qkv[:, 2, k:k + 1].to_broadcast([P, P])).then_inc(bv_ready, 1)
            dve.wait_ge(powered, 1)
            link(dve.tensor_scalar(scale[:, 0:4], pw[:, 0:4], NORM_TO, None, ALU.mult))
            dve.tensor_scalar(gs[:, 0], gam1[:], scale[:, 0:1], None, ALU.mult)
            dve.tensor_scalar(gs[:, 1], gam1[:], scale[:, 1:2], None, ALU.mult)
            dve.tensor_scalar(gs[:, 2], gam1[:], scale[:, 2:3], None, ALU.mult).then_inc(scaled, 1)
            for m in range(2):
                dve.tensor_scalar(bs_qk[:, m], b_qkv[:, m], scale[:, m:m + 1], None, ALU.mult)
            dve.scalar_tensor_tensor(prod[:, 0:1], scale[:, 0:1], float(DH) ** 0.5, scale[:, 1:2],
                                     ALU.mult, ALU.mult)
            link(dve.tensor_tensor(prod[:, 1:2], scale[:, 2:3], scale[:, 3:4], ALU.mult))
            dve.reciprocal(co[:], prod[:, 1:2])
            link(dve.reciprocal(exp_scale[:], prod[:, 0:1]))
            dve.tensor_copy(exp_wide[:], exp_scale[:].to_broadcast([P, TT]))
            dve.tensor_scalar(log_p[:], prod[:, 0:1].to_broadcast([P, TT]), LOG_P, None, ALU.mult).then_inc(scaled, 1)
            dve.wait_ge(scaled, 1)
            for m in range(2):
                for k in range(DK):
                    split_low(m, k)
            dve.tensor_copy(gate_now[:], gates[:, 0:1]).then_inc(gate_set, 1)
            dve.wait_ge(gate_set, 1)
            dve.wait_ge(scaled, 2)
            project(0, True)
            attention(0, True)
            with dve.Fori(1, B) as i:
                project(i, False)
                dve.wait_ge(base_ready, TT * i)
                dve.tensor_copy(gate_now[:], gates[:, bass.ds(i, 1)]).then_inc(gate_set, 1)
                dve.wait_ge(out_ready, TT * (i - 1) + 1)
                dve.tensor_copy(gate_before[:], gates_f[:, bass.ds(i - 1, 1)]).then_inc(gate_set, 1)
                feed_1(i - 1)
                dve.wait_ge(gate_set, 2 * i + 1)
                attention(i, False)
            dve.wait_ge(out_ready, TT * (B - 1) + 1)
            dve.tensor_copy(gate_before[:], gates_f[:, B - 1:B]).then_inc(gate_set, 1)
            dve.wait_ge(gate_set, 2 * B)
            for j in range(QKV):
                tail_step(B, j)
            feed_1(B - 1, last_item=True)
            for t in range(TT):
                output_rows(B - 1, t)


_W = "L0_cond_"
_INS = ["x", "condB_gatescore"] + [_W + n for n in ("Wq", "bq", "Wk", "bk", "Wv", "bv", "Wo", "bo", "W1", "b1", "W2",
                                                   "b2", "gamma1", "beta1", "gamma2", "beta2")]


def kernel(**inputs):
    import numpy as np
    import concourse.bacc as bacc
    from concourse.bass_utils import run_bass_kernel_spmd

    nc = bacc.Bacc("TRN2", target_bir_lowering=False, num_devices=1, dynamic_dma_scratch_size=1024)
    arrays, args = {}, []
    for name in _INS:
        a = np.ascontiguousarray(inputs[name])
        arrays["in_" + name] = a
        args.append(nc.dram_tensor("in_" + name, a.shape, mybir.dt.from_np(a.dtype), kind="ExternalInput").ap())
    shape = inputs["x"].shape
    args.append(nc.dram_tensor("out_0", shape, F32, kind="ExternalOutput").ap())
    build(nc, *args)
    r = run_bass_kernel_spmd(nc, [arrays], core_ids=[0])
    return r.results[0]["out_0"]
```
